# Optimizing a Trainium2 kernel written in Bass

```python
import numpy as np
import jax
import jax.numpy as jnp

def _softmax(x, axis=-1):
    return jax.nn.softmax(x, axis=axis)

def _gelu(x):
    return jax.nn.gelu(x, approximate=True)

def _silu(x):
    return jax.nn.silu(x)

def _sigmoid(x):
    return jax.nn.sigmoid(x)

def _layernorm(x, axis=-1, eps=1e-05):
    m = jnp.mean(x, axis=axis, keepdims=True)
    v = jnp.var(x, axis=axis, keepdims=True)
    return (x - m) / jnp.sqrt(v + eps)

def _scatter_add(tgt, idx, src, axis=0):
    return tgt.at[idx].add(src)

def _segment_sum(src, seg, n):
    return jax.ops.segment_sum(src, seg, n)
kernel_name = 'mk_adaln_d1_jaxref_r8_9634cd'

def setup_inputs(seed: int=0):
    np.random.seed(seed)
    _w = jnp.asarray

    def _L0_attn_setup():
        import jax, jax.numpy as jnp
        import numpy as np
        HIDDEN = 256
        NUM_HEADS = 16
        HEAD_DIM = 128
        WINDOW_SIZE = 64
        NUM_GLOBAL = 16
        SCALING = HEAD_DIM ** (-0.5)

        def _sliding_mask(q_len: int, kv_len: int) -> jnp.ndarray:
            q_pos = jnp.arange(q_len)[:, None]
            kv_pos = jnp.arange(kv_len)[None, :]
            half_window = WINDOW_SIZE // 2
            local = jnp.abs(q_pos - kv_pos) < half_window
            glob = (q_pos < NUM_GLOBAL) | (kv_pos < NUM_GLOBAL)
            mask = local | glob
            return jnp.where(mask, 0.0, -jnp.inf).astype(jnp.float32)
        key = jax.random.key(seed)
        ks = jax.random.split(key, 5)
        std = HIDDEN ** (-0.5)
        hidden_states = jax.random.normal(ks[0], (1, 512, HIDDEN), dtype=jnp.float32)
        Wq = jax.random.normal(ks[1], (HIDDEN, NUM_HEADS * HEAD_DIM), dtype=jnp.float32) * std
        Wk = jax.random.normal(ks[2], (HIDDEN, NUM_HEADS * HEAD_DIM), dtype=jnp.float32) * std
        Wv = jax.random.normal(ks[3], (HIDDEN, NUM_HEADS * HEAD_DIM), dtype=jnp.float32) * std
        Wo = jax.random.normal(ks[4], (NUM_HEADS * HEAD_DIM, HIDDEN), dtype=jnp.float32) * std
        return {'hidden_states': hidden_states, 'Wq': Wq, 'Wk': Wk, 'Wv': Wv, 'Wo': Wo}
    _L0_attn_in = _L0_attn_setup()

    def _L0_ffn_setup():
        import jax, jax.numpy as jnp
        import numpy as np
        DIM_IN = 256
        DIM_HIDDEN = 1024
        key = jax.random.key(seed)
        k_x, k_g, k_u, k_d = jax.random.split(key, 4)
        s_in = 1.0 / np.sqrt(DIM_IN)
        s_hid = 1.0 / np.sqrt(DIM_HIDDEN)
        x = jax.random.normal(k_x, (4, 256, DIM_IN), dtype=jnp.float32)
        w_gate = jax.random.uniform(k_g, (DIM_HIDDEN, DIM_IN), jnp.float32, -s_in, s_in)
        w_up = jax.random.uniform(k_u, (DIM_HIDDEN, DIM_IN), jnp.float32, -s_in, s_in)
        w_down = jax.random.uniform(k_d, (DIM_IN, DIM_HIDDEN), jnp.float32, -s_hid, s_hid)
        return {'x': x, 'w_gate': w_gate, 'w_up': w_up, 'w_down': w_down}
    _L0_ffn_in = _L0_ffn_setup()
    _L0_c = _w((lambda *s: np.random.randn(*s).astype(np.float32) * 0.05)(4, 256))
    _L0_wmod = _w((lambda *s: np.random.randn(*s).astype(np.float32) * 0.05)(256, 6 * 256) * 256 ** (-0.5))
    _d = {'L0_attn_hidden_states': _L0_attn_in['hidden_states'], 'L0_attn_Wq': _L0_attn_in['Wq'], 'L0_attn_Wk': _L0_attn_in['Wk'], 'L0_attn_Wv': _L0_attn_in['Wv'], 'L0_attn_Wo': _L0_attn_in['Wo'], 'L0_ffn_w_gate': _L0_ffn_in['w_gate'], 'L0_ffn_w_up': _L0_ffn_in['w_up'], 'L0_ffn_w_down': _L0_ffn_in['w_down'], 'L0_c': _L0_c, 'L0_wmod': _L0_wmod}
    _x0 = _d['L0_attn_hidden_states']
    _d['L0_attn_hidden_states'] = jax.random.normal(jax.random.fold_in(jax.random.key(seed), 1), (4, 256, 256), dtype=_x0.dtype)
    del _x0
    return _d

def reference(L0_attn_hidden_states, L0_attn_Wq, L0_attn_Wk, L0_attn_Wv, L0_attn_Wo, L0_ffn_w_gate, L0_ffn_w_up, L0_ffn_w_down, L0_c, L0_wmod):

    def _L0_attn_ref(hidden_states, Wq, Wk, Wv, Wo):
        import jax, jax.numpy as jnp
        import numpy as np
        HIDDEN = 256
        NUM_HEADS = 16
        HEAD_DIM = 128
        WINDOW_SIZE = 64
        NUM_GLOBAL = 16
        SCALING = HEAD_DIM ** (-0.5)

        def _sliding_mask(q_len: int, kv_len: int) -> jnp.ndarray:
            q_pos = jnp.arange(q_len)[:, None]
            kv_pos = jnp.arange(kv_len)[None, :]
            half_window = WINDOW_SIZE // 2
            local = jnp.abs(q_pos - kv_pos) < half_window
            glob = (q_pos < NUM_GLOBAL) | (kv_pos < NUM_GLOBAL)
            mask = local | glob
            return jnp.where(mask, 0.0, -jnp.inf).astype(jnp.float32)
        bsz, q_len, _ = hidden_states.shape
        q = (hidden_states @ Wq).reshape(bsz, q_len, NUM_HEADS, HEAD_DIM).transpose(0, 2, 1, 3)
        k = (hidden_states @ Wk).reshape(bsz, q_len, NUM_HEADS, HEAD_DIM).transpose(0, 2, 1, 3)
        v = (hidden_states @ Wv).reshape(bsz, q_len, NUM_HEADS, HEAD_DIM).transpose(0, 2, 1, 3)
        mask = _sliding_mask(q_len, q_len)[None, None]
        scores = jnp.einsum('bhqd,bhkd->bhqk', q, k) * SCALING + mask
        attn = jax.nn.softmax(scores.astype(jnp.float32), axis=-1).astype(q.dtype)
        out = jnp.einsum('bhqk,bhkd->bhqd', attn, v)
        out = out.transpose(0, 2, 1, 3).reshape(bsz, q_len, NUM_HEADS * HEAD_DIM)
        return out @ Wo

    def _L0_ffn_ref(x, w_gate, w_up, w_down):
        import jax, jax.numpy as jnp
        import numpy as np
        DIM_IN = 256
        DIM_HIDDEN = 1024
        gate = jnp.einsum('bsd,hd->bsh', x, w_gate)
        up = jnp.einsum('bsd,hd->bsh', x, w_up)
        gated = jax.nn.silu(gate) * up
        return jnp.einsum('bsh,dh->bsd', gated, w_down)
    x = L0_attn_hidden_states
    mod = (_silu(L0_c) @ L0_wmod).reshape(L0_c.shape[0], 6, 1, -1)
    sa, ca, ga, sb, cb, gb = (mod[:, 0], mod[:, 1], mod[:, 2], mod[:, 3], mod[:, 4], mod[:, 5])
    ga = (2 * (ga >= 0) - 1) * jnp.maximum(jnp.abs(ga), 0.25)
    gb = (2 * (gb >= 0) - 1) * jnp.maximum(jnp.abs(gb), 0.25)
    h = _layernorm(x, axis=-1) * (1 + ca) + sa
    x = x + ga * _L0_attn_ref(h, L0_attn_Wq, L0_attn_Wk, L0_attn_Wv, L0_attn_Wo)
    h = _layernorm(x, axis=-1) * (1 + cb) + sb
    x = x + gb * _L0_ffn_ref(h, L0_ffn_w_gate, L0_ffn_w_up, L0_ffn_w_down)
    return x

_drawn_inputs = setup_inputs


def setup_inputs(seed=0):
    import zlib

    import numpy as np

    out = dict(_drawn_inputs(seed))
    spreads = {}
    factors = {}
    for name, (base, spread) in spreads.items():
        noise = np.random.default_rng([zlib.crc32(name.encode()), seed]).standard_normal(out[name].shape)
        drawn = base * np.exp(spread * noise) if base else spread * noise
        out[name] = jnp.asarray(drawn.astype(out[name].dtype))
    for name, factor in factors.items():
        out[name] = (out[name] * factor).astype(out[name].dtype)
    return out
```

```python
import concourse.bass as bass
from concourse import mybir
from contextlib import ExitStack

F32 = mybir.dt.float32
F32R = mybir.dt.float32r
ALU = mybir.AluOpType
ACT = mybir.ActivationFunctionType

B, S, D = 4, 256, 256
H, DH = 16, 128
F = 1024
P = 128
KT = D // P
NT = B * S // P
HALF = B * S // 2
GLOBAL = 16
WINDOW = 32
SCALE = DH ** -0.5
EPS = 1e-5
MASKED = -1e30
GATE_MIN = 0.25

REACH = P + GLOBAL + WINDOW
FAR = REACH - P

PAIRS = H // 2
UNITS = 2 * B
CHUNKS = 6
NM = F // P
FFN_W = 3 * KT * F
FFN_STEP = FFN_W // PAIRS
FFN_PARTS = 3


def token_order():
    return list(range(GLOBAL, GLOBAL + P)) + list(range(GLOBAL)) + list(range(GLOBAL + P, S))


def adaln_block_kernel(nc, x, wq, wk, wv, wo, wffn, cT, wmod, mask, identity, out):
    ctx = ExitStack()
    with ctx:
        def sb(name, shape, dt=F32):
            return ctx.enter_context(nc.sbuf_tensor(name, shape, dt))

        def sem(name):
            return ctx.enter_context(nc.semaphore(name))

        x_sb = sb("x_sb", [P, NT, D])
        cT_sb = sb("cT_sb", [P, KT, B])
        wmod_sb = sb("wmod_sb", [P, KT, 6 * D])
        mask_sb = sb("mask_sb", [P, REACH + S])
        ident = sb("ident", [P, P])
        silu_c = sb("silu_c", [P, 3, KT * B])
        modT = sb("modT", [P, 4, KT, B])
        gates = sb("gates", [B, 3, 2 * D])
        gates_bc = sb("gates_bc", [P, B, 2, D])
        stats = sb("stats", [P, NT, 6])
        mv = sb("mv", [P, NT, 2])
        rstd = sb("rstd", [P, 3, NT])
        z = sb("z", [P, 4, D])
        haff = sb("haff", [P, 2, KT, S])
        hT = [sb(f"hT_{n}", [P, KT, B * S], F32R) for n in ("hi", "lo")]
        wqk_raw = sb("wqk_raw", [P, 2, KT, 2 * DH])
        wv_raw = sb("wv_raw", [P, KT, 2 * DH])
        wo_raw = sb("wo_raw", [P, 2, D])
        wqk = [sb(f"wqk_{n}", [P, 2, 2, KT, DH], F32R) for n in ("hi", "lo")]
        wv_s = [sb(f"wv_{n}", [P, KT, 2 * DH], F32R) for n in ("hi", "lo")]
        wo_s = [sb(f"wo_{n}", [P, 2, D], F32R) for n in ("hi", "lo")]
        wffn_raw = sb("wffn_raw", [P, FFN_STEP])
        wffn_s = [sb(f"wffn_{n}", [P, FFN_W], F32R) for n in ("hi", "lo")]
        qkT = [sb(f"qkT_{n}", [P, 2, 2, 2, HALF], F32R) for n in ("hi", "lo")]
        v = [sb(f"v_{n}", [P, NT, 2 * DH], F32R) for n in ("hi", "lo")]
        prob = sb("prob", [P, 2, 2, S])
        nmax = sb("nmax", [P, 2, 2])
        rsum = sb("rsum", [P, 2, 2])
        rinv = sb("rinv", [P, 2, 2])
        pT = [sb(f"pT_{n}", [P, 2, S], F32R) for n in ("hi", "lo")]
        oT = [sb(f"oT_{n}", [P, 2, S], F32R) for n in ("hi", "lo")]
        turn = sb("turn", [P, 1])
        acc = sb("acc", [P, NT, D])
        silu_g = wmod_sb[:, 0, 0:2 * HALF].rearrange("p (r n) -> p r n", r=2)
        gated = wmod_sb[:, 1, 0:2 * HALF].rearrange("p (r n) -> p r n", r=2)

        def gated_slot(part, g):
            g = g % 12
            if g < 8:
                return qkT[part][:, g // 4, g // 2 % 2, g % 2, :]
            return v[part][:, 2 * (g - 8):2 * (g - 8) + 2, :].rearrange("p a b -> p (a b)")

        bank = [ctx.enter_context(nc.psum_tensor(f"bank{i}", [P, 512], F32)) for i in range(8)]
        proj_bank, score_bank = bank[0:3], bank[3:5]
        pT_bank, oT_bank, out_bank = bank[5], bank[6], bank[7]

        gates_dram = nc.dram_tensor("gates_scratch", [B, 2 * D], F32).ap()

        x_in = [sem(f"x_in{i}") for i in range(2)]
        const_in = sem("const_in")
        mod_in = sem("mod_in")
        wqk_in, wv_in, wo_in, wffn_in = sem("wqk_in"), sem("wv_in"), sem("wo_in"), sem("wffn_in")
        act_mod = sem("act_mod")
        silu_ready = sem("silu_ready")
        mod_psum = sem("mod_psum")
        modT_ready = sem("modT_ready")
        gates_row = sem("gates_row")
        gates_out = sem("gates_out")
        gates_in = sem("gates_in")
        chain_v = sem("chain_v")
        var_ready, std_ready = sem("var_ready"), sem("std_ready")
        z_ready = sem("z_ready")
        zT_ready = sem("zT_ready")
        haff_ready = sem("haff_ready")
        hT_hi, hT_ready = sem("hT_hi"), sem("hT_ready")
        zeros = sem("zeros")
        wqk_split, wv_split, wo_split = sem("wqk_split"), sem("wv_split"), sem("wo_split")
        wffn_split = sem("wffn_split")
        chain_p = sem("chain_p")
        chunk_ready, chunk_hi, chunk_lo = sem("chunk_ready"), sem("chunk_hi"), sem("chunk_lo")
        scores_ready, masked = sem("scores_ready"), sem("masked")
        exp_done, rinv_ready, softmax_ready = sem("exp_done"), sem("rinv_ready"), sem("softmax_ready")
        pT_ready, pT_hi, pT_lo = sem("pT_ready"), sem("pT_hi"), sem("pT_lo")
        oT_ready, oT_hi, oT_lo = sem("oT_ready"), sem("oT_hi"), sem("oT_lo")
        outp_ready, outp_added = sem("outp_ready"), sem("outp_added")
        gu_ready, silu_done, gated_done = sem("gu_ready"), sem("silu_done"), sem("gated_done")
        gated_hi, gated_lo = sem("gated_hi"), sem("gated_lo")
        down_ready, y_ready, y_out = sem("down_ready"), sem("y_ready"), sem("y_out")

        block = ctx.enter_context(nc.Block())

        def f(ap):
            return ap.bitcast(F32)

        def halves(pe, psum, a, b, first, last):
            (a_hi, a_lo), (b_hi, b_lo) = a, b
            pe.matmul(psum, a_hi, b_hi, start=first, stop=False)
            pe.matmul(psum, a_hi, b_lo, start=False, stop=False)
            return pe.matmul(psum, a_lo, b_hi, start=False, stop=last)

        x_rows = x.rearrange("b s d -> s b d")
        out_rows = out.rearrange("b s d -> s b d")

        def token_tiles(dram, b0, b1):
            return [(slice(0, P), 0, dram[GLOBAL:GLOBAL + P, b0:b1, :]),
                    (slice(0, GLOBAL), 1, dram[0:GLOBAL, b0:b1, :]),
                    (slice(GLOBAL, P), 1, dram[GLOBAL + P:S, b0:b1, :])]

        @block.sync
        def _(sp):
            for half in range(2):
                for parts, odd, rows in token_tiles(x_rows, 2 * half, 2 * half + 2):
                    sp.dma_start(x_sb[parts, 4 * half + odd:4 * half + 4:2, :], rows).then_inc(x_in[half], 16)

            def load_qk(pair):
                for kind, w in enumerate((wq, wk)):
                    sp.dma_start(wqk_raw[:, kind, :, :],
                                 w.rearrange("(k p) n -> p k n", p=P)[:, :, bass.ds(pair * (2 * DH), 2 * DH)])\
                      .then_inc(wqk_in, 16)

            def load_v(pair):
                sp.dma_start(wv_raw[:, :, :],
                             wv.rearrange("(k p) n -> p k n", p=P)[:, :, bass.ds(pair * (2 * DH), 2 * DH)])\
                  .then_inc(wv_in, 16)

            def load_o(pair):
                sp.dma_start(wo_raw[:, :, :],
                             wo.rearrange("(h p) n -> p h n", p=P)[:, bass.ds(pair * 2, 2), :]).then_inc(wo_in, 16)

            def load_ffn(pair):
                sp.dma_start(wffn_raw[:, :], wffn[:, bass.ds(pair * FFN_STEP, FFN_STEP)]).then_inc(wffn_in, 16)

            load_qk(0)
            load_v(0)
            load_o(0)
            load_ffn(0)
            sp.wait_ge(gates_row, 1)
            sp.dma_start(gates_dram, gates[:, 2, :]).then_inc(gates_out, 16)
            sp.wait_ge(gates_out, 16)
            sp.dma_start(gates_bc[:, :, :, :].rearrange("p b g d -> p (b g d)"),
                          gates_dram.rearrange("b n -> (b n)").partition_broadcast(P)).then_inc(gates_in, 16)

            def refill(pair):
                sp.wait_ge(wqk_split, 2 * pair)
                load_qk(pair)
                sp.wait_ge(wv_split, pair)
                load_v(pair)
                sp.wait_ge(wo_split, pair)
                load_o(pair)
                sp.wait_ge(wffn_split, FFN_PARTS * pair)
                load_ffn(pair)

            with sp.Fori(1, PAIRS) as pair:
                refill(pair)

            for b in range(B):
                sp.wait_ge(y_ready, b + 1)
                for parts, odd, rows in token_tiles(out_rows, b, b + 1):
                    sp.dma_start(rows, acc[parts, 2 * b + odd:2 * b + odd + 1, :]).then_inc(y_out, 16)
            sp.wait_ge(y_out, B * 3 * 16)

        @block.gpsimd
        def _(pool):

            per_pair = 4 + FFN_PARTS

            def split_step(raw, hi, lo, done, count):
                pool.tensor_scalar(hi, raw, 1.0, 1.0, ALU.mult, ALU.mult).then_inc(chain_p, 1)
                pool.wait_ge(chain_p, count)
                pool.tensor_tensor(lo, raw, f(hi), ALU.subtract).then_inc(done, 1)

            def split_qk(pair, head, count):
                cols = slice(head * DH, (head + 1) * DH)
                split_step(wqk_raw[:, :, :, cols].rearrange("p a k n -> p (a k) n"),
                           wqk[0][:, head, :, :, :].rearrange("p a k n -> p (a k) n"),
                           wqk[1][:, head, :, :, :].rearrange("p a k n -> p (a k) n"), wqk_split, count)

            def split_v(pair, count):
                split_step(wv_raw[:, :, :], wv_s[0][:, :, :], wv_s[1][:, :, :], wv_split, count)

            def split_o(pair, count):
                split_step(wo_raw[:, :, :], wo_s[0][:, :, :], wo_s[1][:, :, :], wo_split, count)

            def split_ffn(pair, part, count):
                w = FFN_STEP // FFN_PARTS
                raw = wffn_raw[:, part * w:(part + 1) * w]
                hi = wffn_s[0][:, bass.ds(pair * FFN_STEP + part * w, w)]
                lo = wffn_s[1][:, bass.ds(pair * FFN_STEP + part * w, w)]
                pool.tensor_copy(hi, raw).then_inc(chain_p, 1)
                pool.wait_ge(chain_p, count)
                pool.tensor_tensor(lo, raw, f(hi), ALU.subtract).then_inc(wffn_split, 1)

            def normalise(n, i):
                pool.wait_ge(rinv_ready, n + 1)
                r = i % 2
                pool.tensor_tensor(prob[:, r, 0, 0:REACH], prob[:, r, 0, 0:REACH],
                                   rinv[:, r, 0:1].broadcast_to([P, REACH]), ALU.mult)
                pool.tensor_scalar(prob[:, r, 1, :], prob[:, r, 1, :], rinv[:, r, 1:2], 1.0,
                                   ALU.mult, ALU.mult).then_inc(softmax_ready, 1)

            pool.memset(prob[:, :, 0, REACH:S], 0.0)
            for part in range(2):
                last = pool.memset(f(pT[part][:, 1, REACH:S]), 0.0)
            last = pool.memset(acc[:, :, :], 0.0)
            last.then_inc(zeros, 1)
            pool.wait_ge(wqk_in, 32)
            split_qk(0, 0, 1)
            split_qk(0, 1, 2)
            pool.wait_ge(wv_in, 16)
            split_v(0, 3)

            def pair_of_heads(pair, last_pair):
                base = pair * per_pair + 3
                first_chunk = 12 * pair
                for i in range(UNITS):
                    if i == 1 and not last_pair:
                        pool.wait_ge(wqk_in, 32 * (pair + 2))
                        pool.wait_ge(chunk_ready, first_chunk + CHUNKS + 2)
                    if i == 2:
                        pool.wait_ge(wo_in, 16 * (pair + 1))
                        if not (isinstance(pair, int) and pair == 0):
                            pool.wait_ge(outp_ready, B * pair)
                    if i == 3 and not last_pair:
                        pool.wait_ge(chunk_ready, first_chunk + CHUNKS + 4)
                    if i == 4 and not last_pair:
                        pool.wait_ge(wv_in, 16 * (pair + 2))
                        pool.wait_ge(chunk_ready, first_chunk + 2 * CHUNKS)
                    if i == 5:
                        pool.wait_ge(wffn_in, 16 * (pair + 1))
                    normalise(UNITS * pair + i, i)
                    if i == 1 and not last_pair:
                        split_qk(pair + 1, 0, base + 1)
                    if i == 2:
                        split_o(pair, base + (1 if last_pair else 2))
                    if i == 3 and not last_pair:
                        split_qk(pair + 1, 1, base + 3)
                    if i == 4 and not last_pair:
                        split_v(pair + 1, base + 4)
                    if i >= 5:
                        split_ffn(pair, i - 5, base + (1 if last_pair else 4) + i - 4)

            pair_of_heads(0, False)
            with pool.Fori(1, PAIRS - 1) as pair:
                pair_of_heads(pair, False)
            pair_of_heads(PAIRS - 1, True)

        @block.tensor
        def _(pe):
            pe.wait_ge(mod_in, 32)
            pe.wait_ge(silu_ready, 1)
            sc = silu_c[:, 2, :].rearrange("p (k b) -> p k b", b=B)
            for j in range(4):
                for m in range(KT):
                    col = (0, 1, 3, 4)[j] * D + m * P
                    for k in range(KT):
                        last = pe.matmul(bank[5][:, (j * KT + m) * B:(j * KT + m + 1) * B],
                                         wmod_sb[:, k, col:col + P], sc[:, k, :],
                                         start=(k == 0), stop=(k == KT - 1))
            last.then_inc(mod_psum, 1)
            for k in range(KT):
                rows = wmod_sb[:, k, :].rearrange("p (a b d) -> p a b d", a=2, b=3)[:, :, 2, :]
                last = pe.matmul(bank[6][0:B, :], sc[:, k, :], rows, start=(k == 0), stop=(k == KT - 1))
            last.then_inc(mod_psum, 1)

            def transpose_rows(b, count):
                pe.wait_ge(z_ready, count)
                zT = bank[1 + b]
                for k in range(KT):
                    for t in range(2):
                        last = pe.transpose(zT[:, k * S + t * P:k * S + (t + 1) * P],
                                            z[:, 2 * (b % 2) + t, k * P:(k + 1) * P], ident[:, :])
                last.then_inc(zT_ready, 1)

            pe.wait_ge(const_in, 32)
            for b in range(B):
                transpose_rows(b, b + 1)

            def chunk(c, seg_wait, half, i):
                ps = proj_bank[i % 3]
                if not (isinstance(c, int) and c < 3):
                    pe.wait_ge(chunk_lo, c - 2)
                seg_wait()
                if i < 4:
                    head, kind = i // 2, i % 2
                    cols = slice(half * HALF, (half + 1) * HALF)
                    for k in range(KT):
                        last = halves(pe, ps[:, :], [w[:, head, kind, k, :] for w in wqk],
                                      [t[:, k, cols] for t in hT], k == 0, k == KT - 1)
                else:
                    for j in range(2):
                        t = 4 * half + 2 * (i - 4) + j
                        for k in range(KT):
                            last = halves(pe, ps[:, j * 2 * DH:(j + 1) * 2 * DH],
                                          [h[:, k, t * P:(t + 1) * P] for h in hT],
                                          [w[:, k, :] for w in wv_s], k == 0, k == KT - 1)
                last.then_inc(chunk_ready, 1)

            def weights_for(pair, i):
                def wait():
                    if i == 0 or i == 2:
                        pe.wait_ge(wqk_split, 2 * pair + (1 if i == 0 else 2))
                    if i == 4:
                        pe.wait_ge(wv_split, pair + 1)
                return wait

            def scores(n, c0, i):
                half, head, b = i // 4, i % 2, i // 2 % 2
                pe.wait_ge(chunk_lo, c0 + (2 if head == 0 else 4))
                if not (isinstance(n, int) and n < 2):
                    pe.wait_ge(masked, 2 * (n - 1))
                cols = slice(b * S, (b + 1) * S)
                for t in range(2):
                    last = halves(pe, score_bank[i % 2][:, t * S:(t + 1) * S],
                                  [q[:, half, head, 0, b * S + t * P:b * S + (t + 1) * P] for q in qkT],
                                  [q[:, half, head, 1, cols] for q in qkT], True, True)
                last.then_inc(scores_ready, 1)

            def transpose_probs(n, i):
                pe.wait_ge(softmax_ready, n + 1)
                if not (isinstance(n, int) and n < 1):
                    pe.wait_ge(pT_lo, n)
                pr = prob[:, i % 2, :, :]
                pe.transpose(pT_bank[:, 0:P], pr[:, 0, P:S], ident[:, :])
                pe.transpose(pT_bank[:, P:S], pr[:, 1, P:S], ident[:, :])
                pe.transpose(pT_bank[:, S:S + P], pr[:, 0, 0:P], ident[:, :])
                pe.transpose(pT_bank[:, S + P:S + REACH], pr[0:FAR, 1, 0:P], ident[0:FAR, 0:FAR])\
                  .then_inc(pT_ready, 1)

            def attend(n, c0, i):
                half, head, b = i // 4, i % 2, i // 2 % 2
                pe.wait_ge(chunk_lo, c0 + CHUNKS)
                pe.wait_ge(pT_lo, n + 1)
                if not (isinstance(n, int) and n < 1):
                    pe.wait_ge(oT_lo, n)
                t0 = 4 * half + 2 * b
                for slot, t in ((0, 1), (1, 0)):
                    last = halves(pe, oT_bank[:, 0:S],
                                  [w[:, t0 + t, head * DH:(head + 1) * DH] for w in v],
                                  [p[:, slot, :] for p in pT], slot == 0, slot == 1)
                last.then_inc(oT_ready, 1)

            def project_out(u, n_done, pair):
                pe.wait_ge(oT_lo, n_done)
                pe.wait_ge(wo_split, pair + 1)
                if not (isinstance(u, int) and u < 1):
                    pe.wait_ge(outp_added, u)
                for t in range(2):
                    for head in range(2):
                        last = halves(pe, out_bank[:, t * D:(t + 1) * D],
                                      [o[:, head, t * P:(t + 1) * P] for o in oT],
                                      [w[:, head, :] for w in wo_s], head == 0, head == 1)
                last.then_inc(outp_ready, 1)

            pe.wait_ge(hT_ready, 2)
            for i in range(CHUNKS):
                chunk(i, weights_for(0, i), 0, i)
            pe.wait_ge(hT_ready, B)
            pe.wait_ge(modT_ready, 1)
            pe.wait_ge(zeros, 1)

            def pair_of_heads(pair, first_pair, last_pair):
                for i in range(UNITS):
                    n = UNITS * pair + i
                    seg = i // 4
                    c0 = 2 * CHUNKS * pair + CHUNKS * seg
                    new = c0 + CHUNKS
                    new_pair = pair + seg
                    make = not (last_pair and seg == 1)
                    first = (0, 2, 3, 5)[i % 4]
                    scores(n, c0, i)
                    if not (first_pair and i < 2):
                        attend(n - 2, c0 if i % 4 > 1 else c0 - CHUNKS, (i - 2) % UNITS)
                    if make:
                        chunk(new + first, weights_for(new_pair, first), 1 - seg, first)
                    if not (first_pair and i == 0):
                        transpose_probs(n - 1, i - 1)
                    if make and i % 2 == 0:
                        chunk(new + first + 1, weights_for(new_pair, first + 1), 1 - seg, first + 1)
                    if i % 2 == 1 and not (first_pair and i == 1):
                        u = B * pair + (i - 3) // 2
                        project_out(u, n - 1, pair if i > 1 else pair - 1)

            pair_of_heads(0, True, False)
            with pe.Fori(1, PAIRS - 1) as pair:
                pair_of_heads(pair, False, False)
            pair_of_heads(PAIRS - 1, False, True)
            n_end = UNITS * PAIRS
            attend(n_end - 2, 2 * CHUNKS * PAIRS - CHUNKS, UNITS - 2)
            transpose_probs(n_end - 1, 1)
            attend(n_end - 1, 2 * CHUNKS * PAIRS - CHUNKS, UNITS - 1)
            project_out(B * PAIRS - 1, n_end, PAIRS - 1)

            for b in range(B):
                transpose_rows(b, B + b + 1)

            gu_banks = ((bank[0], bank[5]), (bank[6], bank[7]))
            down_banks = ((bank[1], bank[2]), (bank[3], bank[4]))

            def gate_up(half, m):
                g = NM * half + m
                pe.wait_ge(hT_ready, B + 2 * half + 2)
                if g == 0:
                    pe.wait_ge(wffn_split, FFN_PARTS * PAIRS)
                    pe.wait_ge(outp_added, B * PAIRS)
                if g >= 2:
                    pe.wait_ge(gated_done, g - 1)
                for kind in range(2):
                    for k in range(KT):
                        col = (kind * KT + k) * F + m * P
                        last = halves(pe, gu_banks[g % 2][kind][:, :], [w[:, col:col + P] for w in wffn_s],
                                      [t[:, k, half * HALF:(half + 1) * HALF] for t in hT],
                                      k == 0, k == KT - 1)
                    last.then_inc(gu_ready, 1)

            def down(half):
                for t in range(4):
                    ps = down_banks[half][t // 2][:, (t % 2) * D:(t % 2 + 1) * D]
                    for m in range(NM):
                        pe.wait_ge(gated_lo, NM * half + m + 1)
                        col = 2 * KT * F + m * D
                        last = halves(pe, ps, [gated_slot(p, NM * half + m)[:, t * P:(t + 1) * P] for p in (0, 1)],
                                      [w[:, col:col + D] for w in wffn_s], m == 0, m == NM - 1)
                    if t % 2 == 1:
                        last.then_inc(down_ready, 1)

            for half, m in [(0, m) for m in range(NM)] + [(1, 0), (1, 1)]:
                gate_up(half, m)
            down(0)
            for m in range(2, NM):
                gate_up(1, m)
            down(1)

        @block.scalar
        def _(act):
            act.dma_start(cT_sb[:, :, :], cT.rearrange("(k p) b -> p k b", p=P)).then_inc(mod_in, 16)
            act.dma_start(wmod_sb[:, :, :], wmod.rearrange("(k p) n -> p k n", p=P)).then_inc(mod_in, 16)
            act.dma_start(ident[:, :], identity).then_inc(const_in, 16)
            act.dma_start(mask_sb[:, :], mask).then_inc(const_in, 16)
            act.wait_ge(mod_in, 32)
            act.activation(silu_c[:, 0, :], cT_sb[:, :, :].rearrange("p k b -> p (k b)"), ACT.Exp, scale=-1.0)\
               .then_inc(act_mod, 1)

            def roots(half, count):
                act.wait_ge(var_ready, count)
                act.activation(rstd[:, 1, 4 * half:4 * half + 4], rstd[:, 0, 4 * half:4 * half + 4], ACT.Sqrt)\
                   .then_inc(std_ready, 1)

            def h_hi(b, count):
                act.wait_ge(haff_ready, count)
                act.activation(hT[0][:, :, b * S:(b + 1) * S], haff[:, b % 2, :, :], ACT.Copy).then_inc(hT_hi, 1)

            for half in range(2):
                roots(half, half + 1)
            for b in range(B):
                h_hi(b, b + 1)

            def chunk_copy(c, half, i):
                act.wait_ge(chunk_ready, c + 1)
                ps = proj_bank[i % 3]
                if i < 4:
                    dst = qkT[0][:, half, i // 2, i % 2, :]
                else:
                    t = 4 * half + 2 * (i - 4)
                    dst = v[0][:, t:t + 2, :].rearrange("p a b -> p (a b)")
                act.activation(dst, ps[:, :], ACT.Copy).then_inc(chunk_hi, 1)

            def oT_copy(n, i):
                act.wait_ge(oT_ready, n + 1)
                if not (isinstance(n, int) and n < 2):
                    act.wait_ge(outp_ready, (n - i % 2) // 2 if isinstance(n, int) else n_half(n, i))
                act.activation(oT[0][:, i % 2, :], oT_bank[:, 0:S], ACT.Copy).then_inc(oT_hi, 1)

            def n_half(n, i):
                raise AssertionError

            def exps(n, i):
                for t, width in ((0, REACH), (1, S)):
                    act.wait_ge(masked, 2 * n + t + 1)
                    p = prob[:, i % 2, t, 0:width]
                    act.activation(p, p, ACT.Exp, bias=nmax[:, i % 2, t:t + 1], scale=-1.0,
                                   accum_out=rsum[:, i % 2, t:t + 1]).then_inc(exp_done, 1)

            def pT_copy(n):
                act.wait_ge(pT_ready, n + 1)
                act.activation(pT[0][:, :, :].rearrange("p a b -> p (a b)")[:, 0:S + REACH],
                               pT_bank[:, 0:S + REACH], ACT.Copy).then_inc(pT_hi, 1)

            for i in range(CHUNKS):
                chunk_copy(i, 0, i)
            act.wait_ge(zeros, 1)

            def oT_unit(pair, j):
                n = UNITS * pair + j
                act.wait_ge(oT_ready, n + 1)
                if not (isinstance(pair, int) and UNITS * pair + j < 2):
                    act.wait_ge(outp_ready, B * pair + j // 2)
                act.activation(oT[0][:, j % 2, :], oT_bank[:, 0:S], ACT.Copy).then_inc(oT_hi, 1)

            def pair_of_heads(pair, first_pair, last_pair):
                for i in range(UNITS):
                    n = UNITS * pair + i
                    seg = i // 4
                    new = 2 * CHUNKS * pair + CHUNKS * (seg + 1)
                    make = not (last_pair and seg == 1)
                    first = (0, 2, 3, 5)[i % 4]
                    exps(n, i)
                    if not (first_pair and i < 2):
                        oT_unit(pair, i - 2)
                    if make:
                        chunk_copy(new + first, 1 - seg, first)
                    if not (first_pair and i == 0):
                        pT_copy(n - 1)
                    if make and i % 2 == 0:
                        chunk_copy(new + first + 1, 1 - seg, first + 1)

            pair_of_heads(0, True, False)
            with act.Fori(1, PAIRS - 1) as pair:
                pair_of_heads(pair, False, False)
            pair_of_heads(PAIRS - 1, False, True)
            oT_unit(PAIRS, -2)
            pT_copy(UNITS * PAIRS - 1)
            oT_unit(PAIRS, -1)

            for half in range(2):
                roots(half, 2 + half + 1)
            for b in range(B):
                h_hi(b, B + b + 1)

            for g in range(2 * NM):
                act.wait_ge(gu_ready, 2 * g + 1)
                act.activation(silu_g[:, g % 2, :], bank[(0, 6)[g % 2]][:, :], ACT.Silu).then_inc(silu_done, 1)
                act.wait_ge(gated_done, g + 1)
                if g >= 12:
                    act.wait_ge(down_ready, 2)
                act.activation(gated_slot(0, g), gated[:, g % 2, :], ACT.Copy).then_inc(gated_hi, 1)

        @block.vector
        def _(dve):
            chained = [0]

            def link(ins):
                chained[0] += 1
                ins.then_inc(chain_v, 1)
                dve.wait_ge(chain_v, chained[0])

            def ln_stats(half):
                for t in range(4 * half, 4 * half + 4):
                    last = dve.bn_stats(stats[:, t, :], x_sb[:, t, :])
                link(last)
                for t in range(4 * half, 4 * half + 4):
                    last = dve.bn_aggr(mv[:, t, :], stats[:, t, :])
                link(last)
                dve.tensor_scalar(rstd[:, 0, 4 * half:4 * half + 4], mv[:, 4 * half:4 * half + 4, 1], EPS, None,
                                  ALU.add).then_inc(var_ready, 1)

            def ln_rows(half, roots_count, used):
                dve.wait_ge(std_ready, roots_count)
                link(dve.reciprocal(rstd[:, 2, 4 * half:4 * half + 4], rstd[:, 1, 4 * half:4 * half + 4]))
                if used:
                    dve.wait_ge(zT_ready, used)
                for t in range(4):
                    g = 4 * half + t
                    last = dve.tensor_scalar(z[:, t, :], x_sb[:, g, :], mv[:, g, 0:1], rstd[:, 2, g:g + 1],
                                             ALU.subtract, ALU.mult)
                    if t % 2 == 1:
                        last.then_inc(z_ready, 1)

            def modulate(b, shift, count):
                dve.wait_ge(zT_ready, count)
                if count > 2:
                    dve.wait_ge(hT_hi, count - 2)
                for k in range(KT):
                    last = dve.tensor_scalar(haff[:, b % 2, k, :], bank[1 + b][:, k * S:(k + 1) * S],
                                             modT[:, shift + 1, k, b:b + 1], modT[:, shift, k, b:b + 1],
                                             ALU.mult, ALU.add)
                last.then_inc(haff_ready, 1)

            def h_lo(b, count):
                dve.wait_ge(hT_hi, count)
                dve.tensor_tensor(hT[1][:, :, b * S:(b + 1) * S], haff[:, b % 2, :, :],
                                  f(hT[0][:, :, b * S:(b + 1) * S]), ALU.subtract).then_inc(hT_ready, 1)

            dve.wait_ge(act_mod, 1)
            link(dve.tensor_scalar(silu_c[:, 1, :], silu_c[:, 0, :], 1.0, None, ALU.add))
            link(dve.reciprocal(silu_c[:, 0, :], silu_c[:, 1, :]))
            dve.tensor_tensor(silu_c[:, 2, :], silu_c[:, 0, :], cT_sb[:, :, :].rearrange("p k b -> p (k b)"),
                              ALU.mult).then_inc(silu_ready, 1)
            dve.wait_ge(x_in[0], 48)
            ln_stats(0)
            dve.wait_ge(x_in[1], 48)
            ln_stats(1)
            ln_rows(0, 1, 0)
            dve.wait_ge(mod_psum, 1)
            src = bank[5][:, 0:4 * KT * B].rearrange("p (j k b) -> p j k b", j=4, k=KT)
            dve.tensor_copy(modT[:, 0::2, :, :], src[:, 0::2, :, :])
            link(dve.tensor_scalar(modT[:, 1::2, :, :], src[:, 1::2, :, :], 1.0, None, ALU.add))
            modulate(0, 0, 1)
            modulate(1, 0, 2)
            h_lo(0, 1)
            h_lo(1, 2)
            ln_rows(1, 2, 2)
            modulate(2, 0, 3)
            modulate(3, 0, 4)
            h_lo(2, 3)
            h_lo(3, 4)
            dve.wait_ge(mod_psum, 2)
            g_ps = bank[6][0:B, :]
            dve.tensor_scalar(gates[:, 0, :], g_ps, 0.0, 2.0, ALU.is_ge, ALU.mult)
            link(dve.tensor_scalar(gates[:, 2, :], g_ps, -1.0, GATE_MIN, ALU.mult, ALU.max))
            dve.tensor_tensor(gates[:, 1, :], g_ps, gates[:, 2, :], ALU.max).then_inc(modT_ready, 1)
            dve.wait_ge(modT_ready, 1)
            dve.scalar_tensor_tensor(gates[:, 2, :], gates[:, 0, :], -1.0, gates[:, 1, :], ALU.add, ALU.mult)\
               .then_inc(gates_row, 1)

            def chunk_rest(c, half, i):
                dve.wait_ge(chunk_hi, c + 1)
                ps = proj_bank[i % 3]
                if i < 4:
                    hi, lo = (t[:, half, i // 2, i % 2, :] for t in qkT)
                else:
                    t0 = 4 * half + 2 * (i - 4)
                    hi, lo = (t[:, t0:t0 + 2, :].rearrange("p a b -> p (a b)") for t in v)
                dve.tensor_tensor(lo, ps[:, :], f(hi), ALU.subtract).then_inc(chunk_lo, 1)

            def oT_rest(pair, j):
                n = UNITS * pair + j
                dve.wait_ge(oT_hi, n + 1)
                dve.tensor_tensor(oT[1][:, j % 2, :], oT_bank[:, 0:S], f(oT[0][:, j % 2, :]), ALU.subtract)\
                   .then_inc(oT_lo, 1)

            def mask_scores(n, i):
                for t, width in ((0, REACH), (1, S)):
                    dve.tensor_tensor_reduce(out=prob[:, i % 2, t, 0:width],
                                             in0=score_bank[i % 2][:, t * S:t * S + width],
                                             in1=mask_sb[:, t * REACH:t * REACH + width],
                                             scale=-SCALE, scalar=3e38, op0=ALU.add, op1=ALU.min,
                                             accum_out=nmax[:, i % 2, t:t + 1]).then_inc(masked, 1)

            def invert_sums(n, i):
                dve.wait_ge(exp_done, 2 * n + 2)
                dve.reciprocal(rinv[:, i % 2, :], rsum[:, i % 2, :]).then_inc(rinv_ready, 1)

            def pT_rest(n):
                dve.wait_ge(pT_hi, n + 1)
                hi, lo = (t[:, :, :].rearrange("p a b -> p (a b)")[:, 0:S + REACH] for t in pT)
                dve.tensor_tensor(lo, pT_bank[:, 0:S + REACH], f(hi), ALU.subtract).then_inc(pT_lo, 1)

            def add_output(u, b):
                dve.wait_ge(outp_ready, u + 1)
                a = acc[:, 2 * b:2 * b + 2, :]
                dve.tensor_tensor(a, out_bank[:, :].rearrange("p (t d) -> p t d", t=2), a, ALU.add)\
                   .then_inc(outp_added, 1)

            for i in range(CHUNKS):
                chunk_rest(i, 0, i)
            dve.wait_ge(zeros, 1)
            dve.wait_ge(const_in, 32)

            def pair_of_heads(pair, first_pair, last_pair):
                for i in range(UNITS):
                    n = UNITS * pair + i
                    seg = i // 4
                    new = 2 * CHUNKS * pair + CHUNKS * (seg + 1)
                    make = not (last_pair and seg == 1)
                    first = (0, 2, 3, 5)[i % 4]
                    if not (first_pair and i < 2):
                        dve.wait_ge(pT_ready, n - 1)
                    dve.wait_ge(scores_ready, n + 1)
                    dve.memset(turn[:, :], 0.0)
                    mask_scores(n, i)
                    invert_sums(n, i)
                    if not (first_pair and i < 2):
                        oT_rest(pair, i - 2)
                    if make:
                        chunk_rest(new + first, 1 - seg, first)
                    if not (first_pair and i == 0):
                        pT_rest(n - 1)
                    if make and i % 2 == 0:
                        chunk_rest(new + first + 1, 1 - seg, first + 1)
                    if i % 2 == 1 and not (first_pair and i == 1):
                        add_output(B * pair + (i - 3) // 2, (i - 3) // 2 % B)

            pair_of_heads(0, True, False)
            with dve.Fori(1, PAIRS - 1) as pair:
                pair_of_heads(pair, False, False)
            pair_of_heads(PAIRS - 1, False, True)
            oT_rest(PAIRS, -2)
            pT_rest(UNITS * PAIRS - 1)
            oT_rest(PAIRS, -1)

            dve.wait_ge(gates_in, 16)

            def gated_sum(dst, base, value, b, which):
                g = gates_bc[:, b:b + 1, which, :].broadcast_to([P, 2, D])
                link(dve.tensor_tensor(value, value, g, ALU.mult))
                return dve.tensor_tensor(dst, base, value, ALU.add)

            for half in range(2):
                for b in (2 * half, 2 * half + 1):
                    if b == B - 1:
                        add_output(B * PAIRS - 1, B - 1)
                        dve.wait_ge(outp_added, B * PAIRS)
                    tiles = slice(2 * b, 2 * b + 2)
                    link(gated_sum(x_sb[:, tiles, :], x_sb[:, tiles, :], acc[:, tiles, :], b, 0))
                ln_stats(half)
            ln_rows(0, 3, B)
            modulate(0, 2, B + 1)
            modulate(1, 2, B + 2)
            h_lo(0, B + 1)
            h_lo(1, B + 2)
            ln_rows(1, 4, B + 2)
            modulate(2, 2, B + 3)
            modulate(3, 2, B + 4)
            h_lo(2, B + 3)
            h_lo(3, B + 4)

            def finish(b):
                dve.wait_ge(down_ready, b + 1)
                ps = bank[1 + b][:, :].rearrange("p (t d) -> p t d", t=2)
                tiles = slice(2 * b, 2 * b + 2)
                link(dve.tensor_tensor(acc[:, tiles, :], ps, gates_bc[:, b:b + 1, 1, :].broadcast_to([P, 2, D]),
                                       ALU.mult))
                dve.tensor_tensor(acc[:, tiles, :], acc[:, tiles, :], x_sb[:, tiles, :], ALU.add)\
                   .then_inc(y_ready, 1)

            for g in range(2 * NM):
                dve.wait_ge(silu_done, g + 1)
                dve.wait_ge(gu_ready, 2 * g + 2)
                if g >= 2:
                    dve.wait_ge(gated_hi, g - 1)
                dve.tensor_tensor(gated[:, g % 2, :], bank[(5, 7)[g % 2]][:, :], silu_g[:, g % 2, :], ALU.mult)\
                   .then_inc(gated_done, 1)
                dve.wait_ge(gated_hi, g + 1)
                dve.tensor_tensor(gated_slot(1, g), gated[:, g % 2, :], f(gated_slot(0, g)), ALU.subtract)\
                   .then_inc(gated_lo, 1)
                if g == NM + 1:
                    finish(0)
                    finish(1)
            finish(2)
            finish(3)


_OUTS = [((B, S, D), "float32")]


def kernel(**inputs):
    import numpy as _np
    import concourse.bacc as _bacc
    from concourse import mybir as _mybir
    from concourse.bass_utils import run_bass_kernel_spmd as _run

    a = {name.removeprefix("L0_"): _np.asarray(value) for name, value in inputs.items()}
    wffn = _np.concatenate([a["ffn_w_gate"].T.reshape(KT, P, F).transpose(1, 0, 2).reshape(P, -1),
                            a["ffn_w_up"].T.reshape(KT, P, F).transpose(1, 0, 2).reshape(P, -1),
                            a["ffn_w_down"].T.reshape(NM, P, D).transpose(1, 0, 2).reshape(P, -1)], axis=1)
    pos = _np.array(token_order())
    q, k = pos[:, None], pos[None, :]
    seen = (_np.abs(q - k) < WINDOW) | (q < GLOBAL) | (k < GLOBAL)
    full = _np.where(seen, 0.0, MASKED).astype(_np.float32)
    mask = _np.concatenate([full[:P, :REACH], full[P:, :]], axis=1)

    nc = _bacc.Bacc("TRN2", target_bir_lowering=False, num_devices=1)
    named = [("x", a["attn_hidden_states"]), ("wq", a["attn_Wq"]), ("wk", a["attn_Wk"]), ("wv", a["attn_Wv"]),
             ("wo", a["attn_Wo"]), ("wffn", wffn), ("cT", a["c"].T), ("wmod", a["wmod"]), ("mask", mask),
             ("identity", _np.eye(P, dtype=_np.float32))]
    arrays, args = {}, []
    for name, value in named:
        value = _np.ascontiguousarray(value)
        arrays[f"in_{name}"] = value
        args.append(nc.dram_tensor(f"in_{name}", value.shape, _mybir.dt.from_np(value.dtype),
                                   kind="ExternalInput").ap())
    for i, (shape, dtype) in enumerate(_OUTS):
        args.append(nc.dram_tensor(f"out_{i}", shape, _mybir.dt.from_np(_np.dtype(dtype)),
                                   kind="ExternalOutput").ap())
    adaln_block_kernel(nc, *args)
    r = _run(nc, [arrays], core_ids=[0])
    return r.results[0]["out_0"]
```

```python
import concourse.bass as bass
from concourse import mybir
from contextlib import ExitStack

F32 = mybir.dt.float32
F32R = mybir.dt.float32r
I32 = mybir.dt.int32
ALU = mybir.AluOpType
ACT = mybir.ActivationFunctionType

B, S, D = 4, 256, 256
H, DH = 16, 128
F = 1024
P = 128
KT = D // P
NT = B * S // P
HALF = B * S // 2
GLOBAL = 16
WINDOW = 32
SCALE = DH ** -0.5
EPS = 1e-5
MASKED = -1e30
GATE_MIN = 0.25
ROOT_GUESS = float(0x5F3759DF)

REACH = P + GLOBAL + WINDOW
FAR = REACH - P

PAIRS = H // 2
UNITS = 2 * B
CHUNKS = 6
NM = F // P
GROUPS = NM // 2
SLOTS = 12
FFN_W = 3 * KT * F
FFN_STEP = FFN_W // PAIRS
FFN_PARTS = 3


def chunks_of(i, last_pair):
    if last_pair:
        return [i] if i < CHUNKS else []
    return ([0], [1, 2], [3], [4, 5])[i % 4]


def token_order():
    return list(range(GLOBAL, GLOBAL + P)) + list(range(GLOBAL)) + list(range(GLOBAL + P, S))


PAIR_W = 2 * 2 * KT * DH + KT * 2 * DH + 2 * D


def adaln_block_kernel(nc, x, wattn, wffn, cT, wmod, mask, identity, out):
    ctx = ExitStack()
    with ctx:
        def sb(name, shape, dt=F32):
            return ctx.enter_context(nc.sbuf_tensor(name, shape, dt))

        def sem(name):
            return ctx.enter_context(nc.semaphore(name))

        x_sb = sb("x_sb", [P, NT, D])
        cT_sb = sb("cT_sb", [P, KT, B])
        wmod_sb = sb("wmod_sb", [P, KT, 6 * D])
        mask_sb = sb("mask_sb", [P, REACH + S])
        ident = sb("ident", [P, P])
        silu_c = sb("silu_c", [P, 3, KT * B])
        mod_rows = sb("mod_rows", [B, 6 * D])
        modT = sb("modT", [P, 4, KT, B])
        gates_bc = sb("gates_bc", [P, B, 2, D])
        stats = sb("stats", [P, NT, 6])
        mv = sb("mv", [P, NT, 2])
        root = sb("root", [P, 5, NT])
        haff = sb("haff", [P, 2, KT, S])
        hT = [sb(f"hT_{n}", [P, KT, B * S], F32R) for n in ("hi", "lo")]
        wqk_raw = sb("wqk_raw", [P, 2, 2 * KT * DH])
        wv_raw = sb("wv_raw", [P, KT, 2 * DH])
        wo_raw = sb("wo_raw", [P, 2, D])
        wqk = [sb(f"wqk_{n}", [P, 2, 2, KT, DH], F32R) for n in ("hi", "lo")]
        wv_s = [sb(f"wv_{n}", [P, KT, 2 * DH], F32R) for n in ("hi", "lo")]
        wo_s = [sb(f"wo_{n}", [P, 2, D], F32R) for n in ("hi", "lo")]
        wffn_raw = sb("wffn_raw", [P, FFN_STEP])
        wffn_s = [sb(f"wffn_{n}", [P, FFN_W], F32R) for n in ("hi", "lo")]
        qkT = [sb(f"qkT_{n}", [P, 2, 2, 2, HALF], F32R) for n in ("hi", "lo")]
        v = [sb(f"v_{n}", [P, NT, 2 * DH], F32R) for n in ("hi", "lo")]
        prob = sb("prob", [P, 2, 2, S])
        nmax = sb("nmax", [P, 2, 2])
        rsum = sb("rsum", [P, 2, 2])
        rinv = sb("rinv", [P, 2, 2])
        pT = [sb(f"pT_{n}", [P, 2, S], F32R) for n in ("hi", "lo")]
        oT = [sb(f"oT_{n}", [P, 4, S], F32R) for n in ("hi", "lo")]
        turn = sb("turn", [P, 1])
        acc = sb("acc", [P, NT, D])
        tanh_g = wmod_sb[:, 0, 0:2 * HALF].rearrange("p (r n) -> p r n", r=2)
        gated = wmod_sb[:, 1, 0:2 * HALF].rearrange("p (r n) -> p r n", r=2)

        def z_rows(layer, t):
            if layer == 0:
                return acc[:, t, :]
            return wmod_sb[:, t // 2 % 2, 2 * HALF + t % 2 * D:2 * HALF + (t % 2 + 1) * D]

        def gated_slot(part, g):
            g = g % SLOTS
            if g < 8:
                return qkT[part][:, g // 4, g // 2 % 2, g % 2, :]
            return v[part][:, 2 * (g - 8):2 * (g - 8) + 2, :].rearrange("p a b -> p (a b)")

        bank = [ctx.enter_context(nc.psum_tensor(f"bank{i}", [P, 512], F32)) for i in range(8)]
        proj_bank, score_bank = bank[0:3], bank[3:5]
        pT_bank, oT_bank, out_bank = bank[5], bank[6], bank[7]

        zT_bank = [[bank[3], bank[4], bank[5], bank[6]], [bank[0]] * B]
        gu_banks = ((bank[1], bank[2]), (bank[3], bank[4]))
        down_bank = [(bank[5], 0), (bank[5], D), (bank[6], 0), (bank[6], D),
                     (bank[7], 0), (bank[7], D), (bank[5], 0), (bank[6], 0)]

        gates_dram = nc.dram_tensor("gates_scratch", [B, 2 * D], F32).ap()

        x_in = [sem(f"x_in{i}") for i in range(2)]
        ident_in, mask_in, c_in = sem("ident_in"), sem("mask_in"), sem("c_in")
        wmod_in = [sem(f"wmod_in{i}") for i in range(2)]
        wqk_in, wv_in, wo_in, wffn_in = sem("wqk_in"), sem("wv_in"), sem("wo_in"), sem("wffn_in")
        exp_c = sem("exp_c")
        silu_ready = sem("silu_ready")
        mod_psum = sem("mod_psum")
        mod_copied = sem("mod_copied")
        modT_psum, modT_ready = sem("modT_psum"), sem("modT_ready")
        gates_row, gates_out, gates_in = sem("gates_row"), sem("gates_out"), sem("gates_in")
        chain_v = sem("chain_v")
        chain_g = sem("chain_g")
        x2_ready = sem("x2_ready")
        root_ready = sem("root_ready")
        z_ready = sem("z_ready")
        zT_ready = sem("zT_ready")
        haff_ready = sem("haff_ready")
        hT_hi, hT_ready = sem("hT_hi"), sem("hT_ready")
        zeros, acc_zero = sem("zeros"), sem("acc_zero")
        wqk_split, wv_split, wo_split = sem("wqk_split"), sem("wv_split"), sem("wo_split")
        wffn_split = sem("wffn_split")
        chain_p = sem("chain_p")
        chunk_ready, chunk_hi, chunk_lo = sem("chunk_ready"), sem("chunk_hi"), sem("chunk_lo")
        scores_ready, masked = sem("scores_ready"), sem("masked")
        exp_done, rinv_ready, softmax_ready = sem("exp_done"), sem("rinv_ready"), sem("softmax_ready")
        pT_ready, pT_hi, pT_lo = sem("pT_ready"), sem("pT_hi"), sem("pT_lo")
        oT_ready, oT_hi, oT_lo = sem("oT_ready"), sem("oT_hi"), sem("oT_lo")
        outp_ready, outp_added = sem("outp_ready"), sem("outp_added")
        gu_ready, tanh_done, gated_done = sem("gu_ready"), sem("tanh_done"), sem("gated_done")
        gated_hi, gated_lo = sem("gated_hi"), sem("gated_lo")
        down_ready, y_ready, y_out = sem("down_ready"), sem("y_ready"), sem("y_out")

        block = ctx.enter_context(nc.Block())

        def f(ap):
            return ap.bitcast(F32)

        def halves(pe, psum, a, b, first, last):
            (a_hi, a_lo), (b_hi, b_lo) = a, b
            pe.matmul(psum, a_hi, b_hi, start=first, stop=False)
            pe.matmul(psum, a_hi, b_lo, start=False, stop=False)
            return pe.matmul(psum, a_lo, b_hi, start=False, stop=last)

        @block.sync
        def _(sp):
            for half in range(2):
                tiles = slice(4 * half, 4 * half + 4)
                sp.dma_start(x_sb[:, tiles, :], x[:, tiles, :]).then_inc(x_in[half], 16)

            def load(pair, raw, start, width, arrived):
                sp.dma_start(raw, wattn[:, bass.ds(pair * PAIR_W + start, width)]).then_inc(arrived, 16)

            def load_qk(pair):
                load(pair, wqk_raw[:, :, :].rearrange("p a n -> p (a n)"), 0, 4 * KT * DH, wqk_in)

            def load_v(pair):
                load(pair, wv_raw[:, :, :].rearrange("p a n -> p (a n)"), 4 * KT * DH, 2 * KT * DH, wv_in)

            def load_o(pair):
                load(pair, wo_raw[:, :, :].rearrange("p a n -> p (a n)"), 6 * KT * DH, 2 * D, wo_in)

            def load_ffn(pair):
                sp.dma_start(wffn_raw[:, :], wffn[:, bass.ds(pair * FFN_STEP, FFN_STEP)]).then_inc(wffn_in, 16)

            load_qk(0)
            load_v(0)
            load_o(0)
            load_ffn(0)
            with sp.Fori(1, PAIRS) as pair:
                sp.wait_ge(wqk_split, 2 * pair)
                load_qk(pair)
                sp.wait_ge(wv_split, pair)
                load_v(pair)
                sp.wait_ge(wo_split, pair)
                load_o(pair)
                sp.wait_ge(wffn_split, FFN_PARTS * pair)
                load_ffn(pair)

            for t in range(NT):
                sp.wait_ge(y_ready, t + 1)
                sp.dma_start(out[:, t, :], acc[:, t, :]).then_inc(y_out, 16)
            sp.wait_ge(y_out, NT * 16)

        @block.gpsimd
        def _(pool):

            per_pair = 4 + FFN_PARTS

            def split_step(raw, hi, lo, done, count):
                pool.tensor_scalar(hi, raw, 1.0, 1.0, ALU.mult, ALU.mult).then_inc(chain_p, 1)
                pool.wait_ge(chain_p, count)
                pool.tensor_tensor(lo, raw, f(hi), ALU.subtract).then_inc(done, 1)

            def split_qk(pair, head, count):
                split_step(wqk_raw[:, head, :],
                           wqk[0][:, head, :, :, :].rearrange("p a k n -> p (a k n)"),
                           wqk[1][:, head, :, :, :].rearrange("p a k n -> p (a k n)"), wqk_split, count)

            def split_v(pair, count):
                split_step(wv_raw[:, :, :], wv_s[0][:, :, :], wv_s[1][:, :, :], wv_split, count)

            def split_o(pair, count):
                split_step(wo_raw[:, :, :], wo_s[0][:, :, :], wo_s[1][:, :, :], wo_split, count)

            def split_ffn(pair, part, count):
                w = FFN_STEP // FFN_PARTS
                raw = wffn_raw[:, part * w:(part + 1) * w]
                hi = wffn_s[0][:, bass.ds(pair * FFN_STEP + part * w, w)]
                lo = wffn_s[1][:, bass.ds(pair * FFN_STEP + part * w, w)]
                pool.tensor_copy(hi, raw).then_inc(chain_p, 1)
                pool.wait_ge(chain_p, count)
                pool.tensor_tensor(lo, raw, f(hi), ALU.subtract).then_inc(wffn_split, 1)

            def normalise(n, i):
                pool.wait_ge(rinv_ready, n + 1)
                r = i % 2
                pool.tensor_tensor(prob[:, r, 0, 0:REACH], prob[:, r, 0, 0:REACH],
                                   rinv[:, r, 0:1].broadcast_to([P, REACH]), ALU.mult)
                pool.tensor_scalar(prob[:, r, 1, :], prob[:, r, 1, :], rinv[:, r, 1:2], 1.0,
                                   ALU.mult, ALU.mult).then_inc(softmax_ready, 1)

            pool.memset(prob[:, :, 0, REACH:S], 0.0)
            for part in range(2):
                last = pool.memset(f(pT[part][:, 1, REACH:S]), 0.0)
            last.then_inc(zeros, 1)
            pool.wait_ge(wqk_in, 16)
            split_qk(0, 0, 1)
            split_qk(0, 1, 2)
            pool.wait_ge(wv_in, 16)
            split_v(0, 3)
            pool.wait_ge(zT_ready, B)
            pool.memset(acc[:, :, :], 0.0).then_inc(acc_zero, 1)

            def after_attention(b):
                pool.wait_ge(gates_in, 16)
                pool.wait_ge(outp_added, B * (PAIRS - 1) + b + 1)
                tiles = slice(2 * b, 2 * b + 2)
                g = gates_bc[:, b:b + 1, 0, :].broadcast_to([P, 2, D])
                pool.tensor_tensor(acc[:, tiles, :], acc[:, tiles, :], g, ALU.mult).then_inc(chain_g, 1)
                grown[0] += 1
                pool.wait_ge(chain_g, grown[0])
                pool.tensor_tensor(x_sb[:, tiles, :], x_sb[:, tiles, :], acc[:, tiles, :], ALU.add)\
                    .then_inc(x2_ready, 1)

            grown = [0]

            def pair_of_heads(pair, last_pair):
                base = pair * per_pair + 3
                first_chunk = 12 * pair
                done = 0
                ffn_steps = (1, 2, 6) if last_pair else (1, 6, 7)
                for i in range(UNITS):
                    if i == 1:
                        pool.wait_ge(wffn_in, 16 * (pair + 1))
                    if i == 2 and not last_pair:
                        pool.wait_ge(wqk_in, 16 * (pair + 2))
                        pool.wait_ge(chunk_ready, first_chunk + CHUNKS + 2)
                    if i == 3:
                        pool.wait_ge(wo_in, 16 * (pair + 1))
                        if not (isinstance(pair, int) and pair == 0):
                            pool.wait_ge(outp_ready, B * pair)
                    if i == 4 and not last_pair:
                        pool.wait_ge(chunk_ready, first_chunk + CHUNKS + 4)
                    if i == 5 and not last_pair:
                        pool.wait_ge(wv_in, 16 * (pair + 2))
                        pool.wait_ge(chunk_ready, first_chunk + 2 * CHUNKS)
                    normalise(UNITS * pair + i, i)
                    done += 1
                    if i == 2 and not last_pair:
                        split_qk(pair + 1, 0, base + done)
                    elif i == 3:
                        split_o(pair, base + done)
                    elif i == 4 and not last_pair:
                        split_qk(pair + 1, 1, base + done)
                    elif i == 5 and not last_pair:
                        split_v(pair + 1, base + done)
                    elif i in ffn_steps:
                        split_ffn(pair, ffn_steps.index(i), base + done)
                    else:
                        done -= 1
                    if last_pair and i == 4:
                        after_attention(0)

            pair_of_heads(0, False)
            with pool.Fori(1, PAIRS - 1) as pair:
                pair_of_heads(pair, False)
            pair_of_heads(PAIRS - 1, True)
            after_attention(1)
            after_attention(2)
            for g in range(B * GROUPS):
                pool.wait_ge(gated_hi, g + 1)
                pool.tensor_tensor(gated_slot(1, g), gated[:, g % 2, :], f(gated_slot(0, g)), ALU.subtract)\
                    .then_inc(gated_lo, 1)
                if g == 1:
                    after_attention(3)

        @block.tensor
        def _(pe):
            sc = silu_c[:, 2, :].rearrange("p (k b) -> p k b", b=B)

            def modulation(third, ps):
                pe.wait_ge(wmod_in[min(third, 1)], 16)
                for k in range(KT):
                    last = pe.matmul(ps[0:B, :], sc[:, k, :], wmod_sb[:, k, third * 2 * D:(third + 1) * 2 * D],
                                     start=(k == 0), stop=(k == KT - 1))
                last.then_inc(mod_psum, 1)

            def transpose_modulation(ps, j):
                for q in range(2):
                    for m in range(KT):
                        col = (3 * j + q) * D + m * P
                        at = (q * KT + m) * B
                        last = pe.transpose(ps[:, at:at + B], mod_rows[:, col:col + P], ident[0:B, 0:B])
                last.then_inc(modT_psum, 1)

            def transpose_rows(layer, b):
                pe.wait_ge(z_ready, B * layer + b + 1)
                for k in range(KT):
                    for t in range(2):
                        last = pe.transpose(zT_bank[layer][b][:, k * S + t * P:k * S + (t + 1) * P],
                                            z_rows(layer, 2 * b + t)[:, k * P:(k + 1) * P], ident[:, :])
                last.then_inc(zT_ready, 1)

            pe.wait_ge(silu_ready, 1)
            modulation(0, bank[7])
            pe.wait_ge(ident_in, 16)
            pe.wait_ge(mod_copied, 1)
            transpose_modulation(bank[7], 0)
            transpose_rows(0, 0)
            transpose_rows(0, 1)

            def chunk(c, seg_wait, half, i):
                ps = proj_bank[i % 3]
                if not (isinstance(c, int) and c < 3):
                    pe.wait_ge(chunk_lo, c - 2)
                seg_wait()
                if i < 4:
                    head, kind = i // 2, i % 2
                    cols = slice(half * HALF, (half + 1) * HALF)
                    for k in range(KT):
                        last = halves(pe, ps[:, :], [w[:, head, kind, k, :] for w in wqk],
                                      [t[:, k, cols] for t in hT], k == 0, k == KT - 1)
                else:
                    for j in range(2):
                        t = 4 * half + 2 * (i - 4) + j
                        for k in range(KT):
                            last = halves(pe, ps[:, j * 2 * DH:(j + 1) * 2 * DH],
                                          [h[:, k, t * P:(t + 1) * P] for h in hT],
                                          [w[:, k, :] for w in wv_s], k == 0, k == KT - 1)
                last.then_inc(chunk_ready, 1)

            def weights_for(pair, i):
                def wait():
                    if i == 0 or i == 2:
                        pe.wait_ge(wqk_split, 2 * pair + (1 if i == 0 else 2))
                    if i == 4:
                        pe.wait_ge(wv_split, pair + 1)
                return wait

            def scores(n, c0, i):
                half, head, b = i // 4, i % 2, i // 2 % 2
                pe.wait_ge(chunk_lo, c0 + (2 if head == 0 else 4))
                if not (isinstance(n, int) and n < 2):
                    pe.wait_ge(masked, 2 * (n - 1))
                cols = slice(b * S, (b + 1) * S)
                for t in range(2):
                    last = halves(pe, score_bank[i % 2][:, t * S:(t + 1) * S],
                                  [q[:, half, head, 0, b * S + t * P:b * S + (t + 1) * P] for q in qkT],
                                  [q[:, half, head, 1, cols] for q in qkT], True, True)
                last.then_inc(scores_ready, 1)

            def transpose_probs(n, i):
                pe.wait_ge(softmax_ready, n + 1)
                if not (isinstance(n, int) and n < 1):
                    pe.wait_ge(pT_lo, n)
                pr = prob[:, i % 2, :, :]
                pe.transpose(pT_bank[:, 0:P], pr[:, 0, P:S], ident[:, :])
                pe.transpose(pT_bank[:, P:S], pr[:, 1, P:S], ident[:, :])
                pe.transpose(pT_bank[:, S:S + P], pr[:, 0, 0:P], ident[:, :])
                pe.transpose(pT_bank[:, S + P:S + REACH], pr[0:FAR, 1, 0:P], ident[0:FAR, 0:FAR])\
                  .then_inc(pT_ready, 1)

            def attend(n, c0, i):
                half, head, b = i // 4, i % 2, i // 2 % 2
                pe.wait_ge(chunk_lo, c0 + CHUNKS)
                pe.wait_ge(pT_lo, n + 1)
                if not (isinstance(n, int) and n < 1):
                    pe.wait_ge(oT_lo, n)
                t0 = 4 * half + 2 * b
                for slot, t in ((0, 1), (1, 0)):
                    last = halves(pe, oT_bank[:, 0:S],
                                  [w[:, t0 + t, head * DH:(head + 1) * DH] for w in v],
                                  [p[:, slot, :] for p in pT], slot == 0, slot == 1)
                last.then_inc(oT_ready, 1)

            def project_out(u, n_done, pair, i):
                pe.wait_ge(oT_lo, n_done)
                pe.wait_ge(wo_split, pair + 1)
                if not (isinstance(u, int) and u < 1):
                    pe.wait_ge(outp_added, u)
                else:
                    pe.wait_ge(modT_ready, 2)
                for t in range(2):
                    for head in range(2):
                        last = halves(pe, out_bank[:, t * D:(t + 1) * D],
                                      [o[:, i % 4 + head, t * P:(t + 1) * P] for o in oT],
                                      [w[:, head, :] for w in wo_s], head == 0, head == 1)
                last.then_inc(outp_ready, 1)

            pe.wait_ge(hT_ready, 2)
            for i in range(CHUNKS):
                chunk(i, weights_for(0, i), 0, i)
                if i in (3, 4):
                    transpose_rows(0, i - 1)
            pe.wait_ge(zeros, 1)

            def pair_of_heads(pair, first_pair, last_pair):
                for i in range(UNITS):
                    n = UNITS * pair + i
                    seg = i // 4
                    c0 = 2 * CHUNKS * pair + CHUNKS * seg
                    c_seg = 0 if last_pair else seg
                    c_base, c_pair, c_half = 2 * CHUNKS * pair + CHUNKS * (c_seg + 1), pair + c_seg, 1 - c_seg
                    chunks = chunks_of(i, last_pair)
                    scores(n, c0, i)
                    if first_pair and i == 0:
                        pe.wait_ge(hT_ready, B)
                        modulation(1, bank[6])
                        pe.wait_ge(modT_ready, 1)
                        modulation(2, bank[7])
                    if not (first_pair and i < 2):
                        attend(n - 2, c0 if i % 4 > 1 else c0 - CHUNKS, (i - 2) % UNITS)
                    for c in chunks[:1] if not last_pair else ():
                        chunk(c_base + c, weights_for(c_pair, c), c_half, c)
                    if not (first_pair and i == 0):
                        transpose_probs(n - 1, i - 1)
                    if first_pair and i == 2:
                        pe.wait_ge(mod_copied, 3)
                        transpose_modulation(bank[7], 1)
                    for c in chunks if last_pair else chunks[1:]:
                        chunk(c_base + c, weights_for(c_pair, c), c_half, c)
                    if i % 2 == 0 and not (first_pair and i < 4):
                        project_out(B * pair + (i - 4) // 2, n - 2, pair if i >= 4 else pair - 1, i)
                    if last_pair and i == 7:
                        transpose_rows(1, 0)

            pair_of_heads(0, True, False)
            with pe.Fori(1, PAIRS - 1) as pair:
                pair_of_heads(pair, False, False)
            pair_of_heads(PAIRS - 1, False, True)
            n_end = UNITS * PAIRS
            last_chunks = 2 * CHUNKS * PAIRS - CHUNKS
            attend(n_end - 2, last_chunks, UNITS - 2)
            transpose_probs(n_end - 1, 1)
            project_out(B * PAIRS - 2, n_end - 2, PAIRS - 1, 0)

            def gate_up(b, j):
                g = GROUPS * b + j
                pe.wait_ge(hT_ready, B + b + 1)
                if g == 0:
                    pe.wait_ge(wffn_split, FFN_PARTS * PAIRS)
                    pe.wait_ge(chunk_lo, 2 * CHUNKS * PAIRS)
                if g == 1:
                    pe.wait_ge(masked, 2 * UNITS * PAIRS)
                if g >= 2:
                    pe.wait_ge(gated_done, g - 1)
                for kind in range(2):
                    for m in range(2):
                        for k in range(KT):
                            col = (kind * KT + k) * F + (2 * j + m) * P
                            last = halves(pe, gu_banks[g % 2][kind][:, m * S:(m + 1) * S],
                                          [w[:, col:col + P] for w in wffn_s],
                                          [t[:, k, b * S:(b + 1) * S] for t in hT], k == 0, k == KT - 1)
                    last.then_inc(gu_ready, 1)

            def down(b, tiles):
                for t in tiles:
                    ps_bank, at = down_bank[2 * b + t]
                    for m in range(NM):
                        g = GROUPS * b + m // 2
                        pe.wait_ge(gated_lo, g + 1)
                        col = 2 * KT * F + m * D
                        tok = slice(m % 2 * S + t * P, m % 2 * S + (t + 1) * P)
                        last = halves(pe, ps_bank[:, at:at + D], [gated_slot(p, g)[:, tok] for p in (0, 1)],
                                      [w[:, col:col + D] for w in wffn_s], m == 0, m == NM - 1)
                last.then_inc(down_ready, 1)

            gate_up(0, 0)
            attend(n_end - 1, last_chunks, UNITS - 1)
            gate_up(0, 1)
            project_out(B * PAIRS - 1, n_end, PAIRS - 1, 2)
            for b in range(B):
                for j in range(2 if b == 0 else 0, GROUPS):
                    gate_up(b, j)
                    if j == 1 and b < B - 1:
                        down(b - 1, (0, 1))
                    if j == 2 and b < B - 1:
                        pe.wait_ge(haff_ready, B + b + 1)
                        transpose_rows(1, b + 1)
            pe.wait_ge(outp_added, B * PAIRS)
            down(B - 2, (0, 1))
            for t in range(2):
                pe.wait_ge(y_ready, 2 * t + 2)
                down(B - 1, (t,))

        @block.scalar
        def _(act):
            act.dma_start(cT_sb[:, :, :], cT).then_inc(c_in, 16)
            cols = (slice(0, 2 * D), slice(2 * D, 6 * D))
            act.dma_start(wmod_sb[:, :, cols[0]], wmod[:, :, cols[0]]).then_inc(wmod_in[0], 16)
            act.dma_start(ident[:, :], identity).then_inc(ident_in, 16)
            act.dma_start(mask_sb[:, :], mask).then_inc(mask_in, 16)
            act.dma_start(wmod_sb[:, :, cols[1]], wmod[:, :, cols[1]]).then_inc(wmod_in[1], 16)
            act.wait_ge(c_in, 16)
            act.activation(silu_c[:, 0, :], cT_sb[:, :, :].rearrange("p k b -> p (k b)"), ACT.Exp, scale=-1.0)\
               .then_inc(exp_c, 1)

            def modulate(layer, b):
                if layer == 0 and b == 0:
                    act.wait_ge(modT_ready, 1)
                act.wait_ge(zT_ready, B * layer + b + 1)
                if B * layer + b >= 2:
                    act.wait_ge(hT_ready, B * layer + b - 1)
                for k in range(KT):
                    last = act.activation(haff[:, b % 2, k, :], zT_bank[layer][b][:, k * S:(k + 1) * S],
                                          ACT.Identity, scale=modT[:, 2 * layer + 1, k, b:b + 1],
                                          bias=modT[:, 2 * layer, k, b:b + 1])
                last.then_inc(haff_ready, 1)
                act.wait_ge(haff_ready, B * layer + b + 1)
                act.activation(hT[0][:, :, b * S:(b + 1) * S], haff[:, b % 2, :, :], ACT.Copy).then_inc(hT_hi, 1)

            modulate(0, 0)
            modulate(0, 1)

            def chunk_copy(c, half, i):
                act.wait_ge(chunk_ready, c + 1)
                ps = proj_bank[i % 3]
                if i < 4:
                    dst = qkT[0][:, half, i // 2, i % 2, :]
                else:
                    t = 4 * half + 2 * (i - 4)
                    dst = v[0][:, t:t + 2, :].rearrange("p a b -> p (a b)")
                act.activation(dst, ps[:, :], ACT.Copy).then_inc(chunk_hi, 1)

            def exps(n, i):
                for t, width in ((0, REACH), (1, S)):
                    act.wait_ge(masked, 2 * n + t + 1)
                    p = prob[:, i % 2, t, 0:width]
                    act.activation(p, p, ACT.Exp, bias=nmax[:, i % 2, t:t + 1], scale=-1.0,
                                   accum_out=rsum[:, i % 2, t:t + 1]).then_inc(exp_done, 1)

            def pT_copy(n):
                act.wait_ge(pT_ready, n + 1)
                act.activation(pT[0][:, :, :].rearrange("p a b -> p (a b)")[:, 0:S + REACH],
                               pT_bank[:, 0:S + REACH], ACT.Copy).then_inc(pT_hi, 1)

            for i in range(CHUNKS):
                chunk_copy(i, 0, i)
                if i in (3, 4):
                    modulate(0, i - 1)
            act.wait_ge(zeros, 1)

            def oT_unit(pair, j):
                n = UNITS * pair + j
                act.wait_ge(oT_ready, n + 1)
                if not (isinstance(pair, int) and UNITS * pair + j < 4):
                    act.wait_ge(outp_ready, B * pair + j // 2 - 1)
                act.activation(oT[0][:, j % 4, :], oT_bank[:, 0:S], ACT.Copy).then_inc(oT_hi, 1)

            def pair_of_heads(pair, first_pair, last_pair):
                for i in range(UNITS):
                    n = UNITS * pair + i
                    c_seg = 0 if last_pair else i // 4
                    c_base, c_half = 2 * CHUNKS * pair + CHUNKS * (c_seg + 1), 1 - c_seg
                    chunks = chunks_of(i, last_pair)
                    exps(n, i)
                    if not (first_pair and i < 2):
                        oT_unit(pair, i - 2)
                    for c in chunks[:1] if not last_pair else ():
                        chunk_copy(c_base + c, c_half, c)
                    if not (first_pair and i == 0):
                        pT_copy(n - 1)
                    for c in chunks if last_pair else chunks[1:]:
                        chunk_copy(c_base + c, c_half, c)
                    if first_pair and i == 4:
                        act.wait_ge(gates_row, 2)
                        g_rows = mod_rows[:, :].rearrange("b (a c d) -> b a c d", a=2, c=3)[:, :, 2, :]
                        act.dma_start(gates_dram.rearrange("b (g d) -> b g d", g=2), g_rows).then_inc(gates_out, 16)
                    if first_pair and i == 6:
                        act.wait_ge(gates_out, 16)
                        act.dma_start(gates_bc[:, :, :, :].rearrange("p b g d -> p (b g d)"),
                                      gates_dram.rearrange("b n -> (b n)").partition_broadcast(P))\
                           .then_inc(gates_in, 16)

            pair_of_heads(0, True, False)
            with act.Fori(1, PAIRS - 1) as pair:
                pair_of_heads(pair, False, False)
            pair_of_heads(PAIRS - 1, False, True)
            modulate(1, 0)
            oT_unit(PAIRS, -2)
            pT_copy(UNITS * PAIRS - 1)

            for g in range(B * GROUPS):
                act.wait_ge(gu_ready, 2 * g + 1)
                if g >= 2:
                    act.wait_ge(gated_done, g - 1)
                act.activation(tanh_g[:, g % 2, :], gu_banks[g % 2][0][:, :], ACT.Tanh, scale=0.5)\
                   .then_inc(tanh_done, 1)
                if g == 0:
                    oT_unit(PAIRS, -1)
                act.wait_ge(gated_done, g + 1)
                if g >= SLOTS:
                    act.wait_ge(down_ready, 1)
                act.activation(gated_slot(0, g), gated[:, g % 2, :], ACT.Copy).then_inc(gated_hi, 1)
                if g % GROUPS == 2 and g // GROUPS < B - 1:
                    modulate(1, g // GROUPS + 1)

        @block.vector
        def _(dve):
            chained = [0]

            def link(ins):
                chained[0] += 1
                ins.then_inc(chain_v, 1)
                dve.wait_ge(chain_v, chained[0])

            def ln_stats(t0, n):
                for t in range(t0, t0 + n):
                    last = dve.bn_stats(stats[:, t, :], x_sb[:, t, :])
                link(last)
                for t in range(t0, t0 + n):
                    last = dve.bn_aggr(mv[:, t, :], stats[:, t, :])
                link(last)
                dve.tensor_scalar(root[:, 4, t0:t0 + n], mv[:, t0:t0 + n, 0], -1.0, None, ALU.mult)
                link(dve.tensor_scalar(root[:, 0, t0:t0 + n], mv[:, t0:t0 + n, 1], EPS, None, ALU.add))

            def ln_root(t0, n):
                var, y, a, b = (root[:, r, t0:t0 + n] for r in range(4))
                link(dve.tensor_scalar(a.bitcast(I32), var.bitcast(I32), 1, None, ALU.logical_shift_right))
                last = dve.tensor_scalar(y.bitcast(I32), a.bitcast(I32), -1.0, ROOT_GUESS, ALU.mult, ALU.add)
                for _ in range(3):
                    link(last)
                    link(dve.tensor_tensor(a, y, y, ALU.mult))
                    link(dve.scalar_tensor_tensor(b, a, -0.5, var, ALU.mult, ALU.mult))
                    last = dve.scalar_tensor_tensor(y, b, 1.5, y, ALU.add, ALU.mult)
                link(last)

            def ln_rows(layer, t0, n):
                for t in range(t0, t0 + n):
                    last = dve.tensor_scalar(z_rows(layer, t), x_sb[:, t, :], root[:, 4, t:t + 1],
                                             root[:, 1, t:t + 1], ALU.add, ALU.mult)
                    if t % 2 == 1:
                        last.then_inc(z_ready, 1)

            def h_lo(layer, b):
                dve.wait_ge(hT_hi, B * layer + b + 1)
                dve.tensor_tensor(hT[1][:, :, b * S:(b + 1) * S], haff[:, b % 2, :, :],
                                  f(hT[0][:, :, b * S:(b + 1) * S]), ALU.subtract).then_inc(hT_ready, 1)

            def copy_modulation(third, ps):
                dve.wait_ge(mod_psum, third + 1)
                dve.tensor_copy(mod_rows[:, third * 2 * D:(third + 1) * 2 * D], ps[0:B, :]).then_inc(mod_copied, 1)

            def copy_modT(j, ps):
                dve.wait_ge(modT_psum, j + 1)
                src = ps[:, 0:2 * KT * B].rearrange("p (q k b) -> p q k b", q=2, k=KT)
                dve.tensor_copy(modT[:, 2 * j, :, :], src[:, 0, :, :])
                dve.tensor_scalar(modT[:, 2 * j + 1, :, :], src[:, 1, :, :], 1.0, None, ALU.add)\
                   .then_inc(modT_ready, 1)

            def clamp_gate(which):
                g = mod_rows[:, (3 * which + 2) * D:(3 * which + 3) * D]
                sign, size = haff[0:B, 0, which, :], haff[0:B, 1, which, :]
                dve.tensor_scalar(sign, g, 0.0, 2.0, ALU.is_ge, ALU.mult)
                link(dve.tensor_scalar(size, g, -1.0, GATE_MIN, ALU.mult, ALU.max))
                link(dve.tensor_tensor(size, g, size, ALU.max))
                dve.scalar_tensor_tensor(g, sign, -1.0, size, ALU.add, ALU.mult).then_inc(gates_row, 1)

            dve.wait_ge(exp_c, 1)
            link(dve.tensor_scalar(silu_c[:, 1, :], silu_c[:, 0, :], 1.0, None, ALU.add))
            link(dve.reciprocal(silu_c[:, 0, :], silu_c[:, 1, :]))
            dve.tensor_tensor(silu_c[:, 2, :], silu_c[:, 0, :], cT_sb[:, :, :].rearrange("p k b -> p (k b)"),
                              ALU.mult).then_inc(silu_ready, 1)
            dve.wait_ge(x_in[0], 16)
            ln_stats(0, 4)
            copy_modulation(0, bank[7])
            ln_root(0, 4)
            ln_rows(0, 0, 4)
            copy_modT(0, bank[7])
            h_lo(0, 0)
            h_lo(0, 1)

            def chunk_rest(c, half, i):
                dve.wait_ge(chunk_hi, c + 1)
                ps = proj_bank[i % 3]
                if i < 4:
                    hi, lo = (t[:, half, i // 2, i % 2, :] for t in qkT)
                else:
                    t0 = 4 * half + 2 * (i - 4)
                    hi, lo = (t[:, t0:t0 + 2, :].rearrange("p a b -> p (a b)") for t in v)
                dve.tensor_tensor(lo, ps[:, :], f(hi), ALU.subtract).then_inc(chunk_lo, 1)

            def oT_rest(pair, j):
                n = UNITS * pair + j
                dve.wait_ge(oT_hi, n + 1)
                dve.tensor_tensor(oT[1][:, j % 4, :], oT_bank[:, 0:S], f(oT[0][:, j % 4, :]), ALU.subtract)\
                   .then_inc(oT_lo, 1)

            def mask_scores(n, i):
                for t, width in ((0, REACH), (1, S)):
                    dve.tensor_tensor_reduce(out=prob[:, i % 2, t, 0:width],
                                             in0=score_bank[i % 2][:, t * S:t * S + width],
                                             in1=mask_sb[:, t * REACH:t * REACH + width],
                                             scale=-SCALE, scalar=3e38, op0=ALU.add, op1=ALU.min,
                                             accum_out=nmax[:, i % 2, t:t + 1]).then_inc(masked, 1)

            def invert_sums(n, i):
                dve.wait_ge(exp_done, 2 * n + 2)
                dve.reciprocal(rinv[:, i % 2, :], rsum[:, i % 2, :]).then_inc(rinv_ready, 1)

            def pT_rest(n):
                dve.wait_ge(pT_hi, n + 1)
                hi, lo = (t[:, :, :].rearrange("p a b -> p (a b)")[:, 0:S + REACH] for t in pT)
                dve.tensor_tensor(lo, pT_bank[:, 0:S + REACH], f(hi), ALU.subtract).then_inc(pT_lo, 1)

            def add_output(u, b):
                dve.wait_ge(outp_ready, u + 1)
                a = acc[:, 2 * b:2 * b + 2, :]
                dve.tensor_tensor(a, out_bank[:, :].rearrange("p (t d) -> p t d", t=2), a, ALU.add)\
                   .then_inc(outp_added, 1)

            dve.wait_ge(x_in[1], 16)
            ln_stats(4, 4)
            chunk_rest(0, 0, 0)
            ln_root(4, 4)
            chunk_rest(1, 0, 1)
            ln_rows(0, 4, 4)
            chunk_rest(2, 0, 2)
            chunk_rest(3, 0, 3)
            h_lo(0, 2)
            chunk_rest(4, 0, 4)
            h_lo(0, 3)
            chunk_rest(5, 0, 5)
            dve.wait_ge(zeros, 1)
            dve.wait_ge(mask_in, 16)

            def pair_of_heads(pair, first_pair, last_pair):
                for i in range(UNITS):
                    n = UNITS * pair + i
                    c_seg = 0 if last_pair else i // 4
                    c_base, c_half = 2 * CHUNKS * pair + CHUNKS * (c_seg + 1), 1 - c_seg
                    chunks = chunks_of(i, last_pair)
                    if not (first_pair and i < 2):
                        dve.wait_ge(pT_ready, n - 1)
                    dve.wait_ge(scores_ready, n + 1)
                    dve.memset(turn[:, :], 0.0)
                    mask_scores(n, i)
                    invert_sums(n, i)
                    if not (first_pair and i < 2):
                        oT_rest(pair, i - 2)
                    if first_pair and i == 0:
                        copy_modulation(1, bank[6])
                        copy_modulation(2, bank[7])
                    for c in chunks[:1] if not last_pair else ():
                        chunk_rest(c_base + c, c_half, c)
                    if not (first_pair and i == 0):
                        pT_rest(n - 1)
                    for c in chunks if last_pair else chunks[1:]:
                        chunk_rest(c_base + c, c_half, c)
                    if first_pair and i == 2:
                        copy_modT(1, bank[7])
                        clamp_gate(0)
                    if first_pair and i == 3:
                        clamp_gate(1)
                        dve.wait_ge(acc_zero, 1)
                    if i % 2 == 0 and not (first_pair and i < 4):
                        add_output(B * pair + (i - 4) // 2, (i - 4) // 2 % B)
                    if last_pair and i == 5:
                        dve.wait_ge(x2_ready, 1)
                        ln_stats(0, 2)
                    if last_pair and i == 6:
                        ln_root(0, 2)
                        ln_rows(1, 0, 2)

            pair_of_heads(0, True, False)
            with dve.Fori(1, PAIRS - 1) as pair:
                pair_of_heads(pair, False, False)
            pair_of_heads(PAIRS - 1, False, True)
            oT_rest(PAIRS, -2)
            h_lo(1, 0)
            pT_rest(UNITS * PAIRS - 1)
            add_output(B * PAIRS - 2, 2)

            def finish(t, n):
                ps_bank, at = down_bank[t]
                ps = ps_bank[:, at:at + n * D].rearrange("p (t d) -> p t d", t=n)
                tiles = slice(t, t + n)
                g = gates_bc[:, t // 2:t // 2 + 1, 1, :].broadcast_to([P, n, D])
                link(dve.tensor_tensor(acc[:, tiles, :], ps, g, ALU.mult))
                dve.tensor_tensor(acc[:, tiles, :], acc[:, tiles, :], x_sb[:, tiles, :], ALU.add)\
                   .then_inc(y_ready, n)

            for g in range(B * GROUPS):
                b, j = g // GROUPS, g % GROUPS
                dve.wait_ge(tanh_done, g + 1)
                t = tanh_g[:, g % 2, :]
                link(dve.scalar_tensor_tensor(t, t, 1.0, gu_banks[g % 2][0][:, :], ALU.add, ALU.mult))
                dve.wait_ge(gu_ready, 2 * g + 2)
                if g >= 2:
                    dve.wait_ge(gated_lo, g - 1)
                dve.scalar_tensor_tensor(gated[:, g % 2, :], t, 0.5, gu_banks[g % 2][1][:, :],
                                         ALU.mult, ALU.mult).then_inc(gated_done, 1)
                if g == 0:
                    oT_rest(PAIRS, -1)
                    dve.wait_ge(x2_ready, 2)
                    ln_stats(2, 2)
                    ln_root(2, 2)
                    ln_rows(1, 2, 2)
                if g == 1:
                    add_output(B * PAIRS - 1, 3)
                if g == GROUPS + 1:
                    dve.wait_ge(x2_ready, B)
                    ln_stats(4, 4)
                    ln_root(4, 4)
                    dve.wait_ge(zT_ready, B + 2)
                    ln_rows(1, 4, 4)
                if j == 2 and b < B - 1:
                    h_lo(1, b + 1)
                    if b > 0:
                        dve.wait_ge(down_ready, b)
                        finish(2 * b - 2, 2)
            dve.wait_ge(down_ready, B - 1)
            finish(NT - 4, 2)
            for t in (NT - 2, NT - 1):
                dve.wait_ge(down_ready, B + t - (NT - 2))
                finish(t, 1)


_OUTS = [((P, NT, D), "float32")]


def kernel(**inputs):
    import numpy as _np
    import concourse.bacc as _bacc
    from concourse import mybir as _mybir
    from concourse.bass_utils import run_bass_kernel_spmd as _run

    a = {name.removeprefix("L0_"): _np.asarray(value) for name, value in inputs.items()}
    def by_partition(w):
        return w.reshape(-1, P, w.shape[1]).transpose(1, 0, 2)

    qk = _np.stack([by_partition(a["attn_Wq"]), by_partition(a["attn_Wk"])], axis=1)
    qk = qk.reshape(P, 2, KT, PAIRS, 2, DH).transpose(0, 3, 4, 1, 2, 5).reshape(P, PAIRS, -1)
    wv = by_partition(a["attn_Wv"]).reshape(P, KT, PAIRS, 2 * DH).transpose(0, 2, 1, 3).reshape(P, PAIRS, -1)
    wo = by_partition(a["attn_Wo"]).reshape(P, PAIRS, 2 * D)
    wattn = _np.concatenate([qk, wv, wo], axis=2).reshape(P, -1)
    wffn = _np.concatenate([by_partition(w.T).reshape(P, -1)
                            for w in (a["ffn_w_gate"], a["ffn_w_up"], a["ffn_w_down"])], axis=1)
    order = _np.array(token_order())
    x = a["attn_hidden_states"][:, order, :].reshape(NT, P, D).transpose(1, 0, 2)
    q, k = order[:, None], order[None, :]
    seen = (_np.abs(q - k) < WINDOW) | (q < GLOBAL) | (k < GLOBAL)
    full = _np.where(seen, 0.0, MASKED).astype(_np.float32)
    mask = _np.concatenate([full[:P, :REACH], full[P:, :]], axis=1)

    nc = _bacc.Bacc("TRN2", target_bir_lowering=False, num_devices=1)
    named = [("x", x), ("wattn", wattn), ("wffn", wffn), ("cT", by_partition(a["c"].T)),
             ("wmod", by_partition(a["wmod"])), ("mask", mask), ("identity", _np.eye(P, dtype=_np.float32))]
    arrays, args = {}, []
    for name, value in named:
        value = _np.ascontiguousarray(value)
        arrays[f"in_{name}"] = value
        args.append(nc.dram_tensor(f"in_{name}", value.shape, _mybir.dt.from_np(value.dtype),
                                   kind="ExternalInput").ap())
    for i, (shape, dtype) in enumerate(_OUTS):
        args.append(nc.dram_tensor(f"out_{i}", shape, _mybir.dt.from_np(_np.dtype(dtype)),
                                   kind="ExternalOutput").ap())
    adaln_block_kernel(nc, *args)
    r = _run(nc, [arrays], core_ids=[0])
    y = _np.empty((B, S, D), _np.float32)
    y[:, order, :] = _np.asarray(r.results[0]["out_0"]).transpose(1, 0, 2).reshape(B, S, D)
    return y
```

```python
import concourse.bass as bass
from concourse import mybir
from contextlib import ExitStack

F32 = mybir.dt.float32
F32R = mybir.dt.float32r
I32 = mybir.dt.int32
ALU = mybir.AluOpType
ACT = mybir.ActivationFunctionType

B, S, D = 4, 256, 256
H, DH = 16, 128
F = 1024
P = 128
KT = D // P
NT = B * S // P
HALF = B * S // 2
GLOBAL = 16
WINDOW = 32
SCALE = DH ** -0.5
EPS = 1e-5
MASKED = -1e30
GATE_MIN = 0.25
ROOT_GUESS = float(0x5F3759DF)

REACH = P + GLOBAL + WINDOW
FAR = REACH - P

PAIRS = H // 2
UNITS = 2 * B
CHUNKS = 6
NM = F // P
GROUPS = NM // 2
SLOTS = 12
FFN_W = 3 * KT * F
FFN_STEP = FFN_W // PAIRS
FFN_PARTS = 3


def chunks_of(i, first_pair, last_pair):
    if last_pair:
        return ([i] if i < CHUNKS else []), 0
    return ([0], [1, 2], [3], [4, 5])[i % 4], (0 if first_pair and i < 4 else 1)


def token_order():
    return list(range(GLOBAL, GLOBAL + P)) + list(range(GLOBAL)) + list(range(GLOBAL + P, S))


PAIR_W = 2 * 2 * KT * DH + KT * 2 * DH + 2 * D


def adaln_block_kernel(nc, x, wattn, wffn, cT, wmod, mask, identity, out):
    ctx = ExitStack()
    with ctx:
        def sb(name, shape, dt=F32):
            return ctx.enter_context(nc.sbuf_tensor(name, shape, dt))

        def sem(name):
            return ctx.enter_context(nc.semaphore(name))

        x_sb = sb("x_sb", [P, NT, D])
        cT_sb = sb("cT_sb", [P, KT, B])
        wmod_sb = sb("wmod_sb", [P, KT, 6 * D])
        mask_sb = sb("mask_sb", [P, REACH + S])
        ident = sb("ident", [P, P])
        silu_c = sb("silu_c", [P, 3, KT * B])
        mod_rows = sb("mod_rows", [B, 6 * D])
        modT = sb("modT", [P, 4, KT, B])
        gate_tmp = sb("gate_tmp", [B, 2, D])
        gates_bc = sb("gates_bc", [P, B, 2, D])
        stats = sb("stats", [P, NT, 6])
        mv = sb("mv", [P, NT, 2])
        root = sb("root", [P, 5, NT])
        haff = sb("haff", [P, 2, KT, S])
        hT = [sb(f"hT_{n}", [P, KT, B * S], F32R) for n in ("hi", "lo")]
        wqk_raw = sb("wqk_raw", [P, 2, 2 * KT * DH])
        wv_raw = sb("wv_raw", [P, KT, 2 * DH])
        wo_raw = sb("wo_raw", [P, 2, D])
        wqk = [sb(f"wqk_{n}", [P, 2, 2, KT, DH], F32R) for n in ("hi", "lo")]
        wv_s = [sb(f"wv_{n}", [P, KT, 2 * DH], F32R) for n in ("hi", "lo")]
        wo_s = [sb(f"wo_{n}", [P, 2, D], F32R) for n in ("hi", "lo")]
        wffn_raw = sb("wffn_raw", [P, FFN_STEP])
        wffn_s = [sb(f"wffn_{n}", [P, FFN_W], F32R) for n in ("hi", "lo")]
        qkT = [sb(f"qkT_{n}", [P, 2, 2, 2, HALF], F32R) for n in ("hi", "lo")]
        v = [sb(f"v_{n}", [P, NT, 2 * DH], F32R) for n in ("hi", "lo")]
        prob = sb("prob", [P, 2, 2, S])
        nmax = sb("nmax", [P, 2, 2])
        rsum = sb("rsum", [P, 2, 2])
        rinv = sb("rinv", [P, 2, 2])
        pT = [sb(f"pT_{n}", [P, 2, S], F32R) for n in ("hi", "lo")]
        oT = [sb(f"oT_{n}", [P, 4, S], F32R) for n in ("hi", "lo")]
        turn = sb("turn", [P, 1])
        acc = sb("acc", [P, NT, D])
        tanh_g = wmod_sb[:, 0, 0:2 * HALF].rearrange("p (r n) -> p r n", r=2)
        gated = wmod_sb[:, 1, 0:2 * HALF].rearrange("p (r n) -> p r n", r=2)

        def z_rows(layer, t):
            if layer == 0:
                return acc[:, t, :]
            return wmod_sb[:, t // 2 % 2, 2 * HALF + t % 2 * D:2 * HALF + (t % 2 + 1) * D]

        def gated_slot(part, g):
            g = g % SLOTS
            if g < 8:
                return qkT[part][:, g // 4, g // 2 % 2, g % 2, :]
            return v[part][:, 2 * (g - 8):2 * (g - 8) + 2, :].rearrange("p a b -> p (a b)")

        bank = [ctx.enter_context(nc.psum_tensor(f"bank{i}", [P, 512], F32)) for i in range(8)]
        proj_bank, score_bank = bank[0:3], bank[3:5]
        pT_bank, oT_bank, out_bank = bank[5], bank[6], bank[7]

        zT_bank = [[bank[3], bank[4], bank[5], bank[6]], [bank[0]] * B]
        gu_banks = ((bank[1], bank[2]), (bank[3], bank[4]))
        down_bank = [(bank[5], 0), (bank[5], D), (bank[6], 0), (bank[6], D),
                     (bank[7], 0), (bank[7], D), (bank[5], 0), (bank[6], 0)]

        gates_dram = nc.dram_tensor("gates_scratch", [B, 2 * D], F32).ap()

        x_in = [sem(f"x_in{i}") for i in range(3)]
        ident_in, mask_in, c_in = sem("ident_in"), sem("mask_in"), sem("c_in")
        wmod_in = [sem(f"wmod_in{i}") for i in range(2)]
        wqk_in, wv_in, wo_in, wffn_in = sem("wqk_in"), sem("wv_in"), sem("wo_in"), sem("wffn_in")
        exp_c, silu_ready = sem("exp_c"), sem("silu_ready")
        mod_psum, mod_copied = sem("mod_psum"), sem("mod_copied")
        modT_psum, modT_ready = sem("modT_psum"), sem("modT_ready")
        gates_row = sem("gates_row")
        gates_out, gates_in = sem("gates_out"), sem("gates_in")
        chain_v = sem("chain_v")
        chain_g = sem("chain_g")
        chain_p = sem("chain_p")
        x2_ready = sem("x2_ready")
        z_ready = sem("z_ready")
        zT_ready = sem("zT_ready")
        haff_ready = sem("haff_ready")
        hT_hi, hT_ready = sem("hT_hi"), sem("hT_ready")
        zeros, acc_zero = sem("zeros"), sem("acc_zero")
        wqk_split = sem("wqk_split")
        wv_split, wo_split = sem("wv_split"), sem("wo_split")
        wffn_split = sem("wffn_split")
        chunk_ready, chunk_hi, chunk_lo = sem("chunk_ready"), sem("chunk_hi"), sem("chunk_lo")
        scores_ready, masked, exp_done = sem("scores_ready"), sem("masked"), sem("exp_done")
        rinv_ready, softmax_ready = sem("rinv_ready"), sem("softmax_ready")
        pT_ready, pT_hi, pT_lo = sem("pT_ready"), sem("pT_hi"), sem("pT_lo")
        oT_ready, oT_hi, oT_lo = sem("oT_ready"), sem("oT_hi"), sem("oT_lo")
        outp_ready, outp_added = sem("outp_ready"), sem("outp_added")
        gu_ready = sem("gu_ready")
        tanh_done, gated_done = sem("tanh_done"), sem("gated_done")
        gated_hi, gated_lo = sem("gated_hi"), sem("gated_lo")
        down_ready = sem("down_ready")
        y_ready, y_out = sem("y_ready"), sem("y_out")

        block = ctx.enter_context(nc.Block())

        def f(ap):
            return ap.bitcast(F32)

        def halves(pe, psum, a, b, first, last):
            (a_hi, a_lo), (b_hi, b_lo) = a, b
            pe.matmul(psum, a_hi, b_hi, start=first, stop=False)
            pe.matmul(psum, a_hi, b_lo, start=False, stop=False)
            return pe.matmul(psum, a_lo, b_hi, start=False, stop=last)

        @block.sync
        def _(sp):
            def load_x(n, tiles):
                sp.dma_start(x_sb[:, tiles, :], x[:, tiles, :]).then_inc(x_in[n], 16)

            def load(pair, raw, start, width, arrived):
                sp.dma_start(raw, wattn[:, bass.ds(pair * PAIR_W + start, width)]).then_inc(arrived, 16)

            def load_qk(pair):
                load(pair, wqk_raw[:, :, :].rearrange("p a n -> p (a n)"), 0, 4 * KT * DH, wqk_in)

            def load_v(pair):
                load(pair, wv_raw[:, :, :].rearrange("p a n -> p (a n)"), 4 * KT * DH, 2 * KT * DH, wv_in)

            def load_o(pair):
                load(pair, wo_raw[:, :, :].rearrange("p a n -> p (a n)"), 6 * KT * DH, 2 * D, wo_in)

            def load_ffn(pair):
                sp.dma_start(wffn_raw[:, :], wffn[:, bass.ds(pair * FFN_STEP, FFN_STEP)]).then_inc(wffn_in, 16)

            sp.dma_start(cT_sb[:, :, :], cT).then_inc(c_in, 16)
            load_x(0, slice(0, 2))
            load_x(1, slice(2, 4))
            load_qk(0)
            load_x(2, slice(4, NT))
            load_v(0)
            load_o(0)
            load_ffn(0)

            with sp.Fori(1, PAIRS) as pair:
                sp.wait_ge(wqk_split, 2 * pair)
                load_qk(pair)
                sp.wait_ge(wv_split, pair)
                load_v(pair)
                sp.wait_ge(wo_split, pair)
                load_o(pair)
                sp.wait_ge(wffn_split, FFN_PARTS * pair)
                load_ffn(pair)

            for t in range(NT):
                sp.wait_ge(y_ready, t + 1)
                sp.dma_start(out[:, t, :], acc[:, t, :]).then_inc(y_out, 16)
            sp.wait_ge(y_out, NT * 16)

        @block.gpsimd
        def _(pool):
            per_pair = 4 + FFN_PARTS

            def split_step(raw, hi, lo, done, count):
                pool.tensor_scalar(hi, raw, 1.0, 1.0, ALU.mult, ALU.mult).then_inc(chain_p, 1)
                pool.wait_ge(chain_p, count)
                pool.tensor_tensor(lo, raw, f(hi), ALU.subtract).then_inc(done, 1)

            def split_qk(pair, head, count):
                split_step(wqk_raw[:, head, :],
                           wqk[0][:, head, :, :, :].rearrange("p a k n -> p (a k n)"),
                           wqk[1][:, head, :, :, :].rearrange("p a k n -> p (a k n)"), wqk_split, count)

            def split_v(pair, count):
                split_step(wv_raw[:, :, :], wv_s[0][:, :, :], wv_s[1][:, :, :], wv_split, count)

            def split_o(pair, count):
                split_step(wo_raw[:, :, :], wo_s[0][:, :, :], wo_s[1][:, :, :], wo_split, count)

            def split_ffn(pair, part, count):
                w = FFN_STEP // FFN_PARTS
                raw = wffn_raw[:, part * w:(part + 1) * w]
                hi = wffn_s[0][:, bass.ds(pair * FFN_STEP + part * w, w)]
                lo = wffn_s[1][:, bass.ds(pair * FFN_STEP + part * w, w)]
                pool.tensor_copy(hi, raw).then_inc(chain_p, 1)
                pool.wait_ge(chain_p, count)
                pool.tensor_tensor(lo, raw, f(hi), ALU.subtract).then_inc(wffn_split, 1)

            def normalise(n, i):
                pool.wait_ge(rinv_ready, n + 1)
                r = i % 2
                pool.tensor_tensor(prob[:, r, 0, 0:REACH], prob[:, r, 0, 0:REACH],
                                   rinv[:, r, 0:1].broadcast_to([P, REACH]), ALU.mult)
                pool.tensor_scalar(prob[:, r, 1, :], prob[:, r, 1, :], rinv[:, r, 1:2], 1.0,
                                   ALU.mult, ALU.mult).then_inc(softmax_ready, 1)

            chained = [0]

            def link(ins):
                chained[0] += 1
                ins.then_inc(chain_g, 1)
                pool.wait_ge(chain_g, chained[0])

            def clamp_gate(which):
                pool.wait_ge(mod_copied, which + 1)
                if which == 1:
                    pool.wait_ge(gates_row, 1)
                g = mod_rows[:, (3 * which + 2) * D:(3 * which + 3) * D]
                sign, size = gate_tmp[:, 0, :], gate_tmp[:, 1, :]
                link(pool.tensor_scalar(sign, g, 0.0, -0.5, ALU.is_ge, ALU.add))
                link(pool.tensor_tensor(size, sign, g, ALU.mult))
                link(pool.tensor_scalar(size, size, GATE_MIN / 2, 4.0, ALU.max, ALU.mult))
                pool.tensor_tensor(g, sign, size, ALU.mult).then_inc(gates_row, 1)

            def h_lo(b):
                pool.wait_ge(hT_hi, b + 1)
                pool.tensor_tensor(hT[1][:, :, b * S:(b + 1) * S], haff[:, b % 2, :, :],
                                   f(hT[0][:, :, b * S:(b + 1) * S]), ALU.subtract).then_inc(hT_ready, 1)

            pool.memset(prob[:, :, 0, REACH:S], 0.0)
            for part in range(2):
                last = pool.memset(f(pT[part][:, 1, REACH:S]), 0.0)
            last.then_inc(zeros, 1)
            pool.wait_ge(wqk_in, 16)
            split_qk(0, 0, 1)
            split_qk(0, 1, 2)
            pool.wait_ge(wv_in, 16)
            split_v(0, 3)
            clamp_gate(0)
            pool.wait_ge(hT_ready, 2)
            h_lo(2)
            h_lo(3)
            pool.memset(acc[:, :, :], 0.0).then_inc(acc_zero, 1)

            def after_attention(b):
                pool.wait_ge(gates_in, 16)
                pool.wait_ge(outp_added, B * (PAIRS - 1) + b + 1)
                tiles = slice(2 * b, 2 * b + 2)
                g = gates_bc[:, b:b + 1, 0, :].broadcast_to([P, 2, D])
                link(pool.tensor_tensor(acc[:, tiles, :], acc[:, tiles, :], g, ALU.mult))
                pool.tensor_tensor(x_sb[:, tiles, :], x_sb[:, tiles, :], acc[:, tiles, :], ALU.add)\
                    .then_inc(x2_ready, 1)

            def pair_of_heads(pair, first_pair, last_pair):
                base = pair * per_pair + 3
                first_chunk = 2 * CHUNKS * pair
                done = 0
                ffn_steps = (1, 2, 6) if last_pair else (1, 6, 7)
                for i in range(UNITS):
                    if i == 1:
                        pool.wait_ge(wffn_in, 16 * (pair + 1))
                    if i == 2 and not last_pair:
                        pool.wait_ge(wqk_in, 16 * (pair + 2))
                        pool.wait_ge(chunk_ready, first_chunk + CHUNKS + 2)
                    if i == 3:
                        pool.wait_ge(wo_in, 16 * (pair + 1))
                        if not first_pair:
                            pool.wait_ge(outp_ready, B * pair)
                    if i == 4 and not last_pair:
                        pool.wait_ge(chunk_ready, first_chunk + CHUNKS + 4)
                    if i == 5 and not last_pair:
                        pool.wait_ge(wv_in, 16 * (pair + 2))
                        pool.wait_ge(chunk_ready, first_chunk + 2 * CHUNKS)
                    normalise(UNITS * pair + i, i)
                    done += 1
                    if i == 2 and not last_pair:
                        split_qk(pair + 1, 0, base + done)
                    elif i == 3:
                        split_o(pair, base + done)
                    elif i == 4 and not last_pair:
                        split_qk(pair + 1, 1, base + done)
                    elif i == 5 and not last_pair:
                        split_v(pair + 1, base + done)
                    elif i in ffn_steps:
                        split_ffn(pair, ffn_steps.index(i), base + done)
                    else:
                        done -= 1
                    if first_pair and i == 0:
                        clamp_gate(1)
                    if last_pair and i == 4:
                        after_attention(0)

            pair_of_heads(0, True, False)
            with pool.Fori(1, PAIRS - 1) as pair:
                pair_of_heads(pair, False, False)
            pair_of_heads(PAIRS - 1, False, True)
            after_attention(1)
            after_attention(2)
            for g in range(B * GROUPS):
                pool.wait_ge(gated_hi, g + 1)
                pool.tensor_tensor(gated_slot(1, g), gated[:, g % 2, :], f(gated_slot(0, g)), ALU.subtract)\
                    .then_inc(gated_lo, 1)
                if g == 1:
                    after_attention(3)

        @block.tensor
        def _(pe):
            sc = silu_c[:, 2, :].rearrange("p (k b) -> p k b", b=B)

            def modulation_T(ps):
                pe.wait_ge(wmod_in[0], 16)
                for q in range(2):
                    for m in range(KT):
                        at = (q * KT + m) * B
                        for k in range(KT):
                            last = pe.matmul(ps[:, at:at + B], wmod_sb[:, k, q * D + m * P:q * D + (m + 1) * P],
                                             sc[:, k, :], start=(k == 0), stop=(k == KT - 1))
                last.then_inc(modT_psum, 1)

            def modulation(third, ps):
                pe.wait_ge(wmod_in[1], 16)
                for k in range(KT):
                    last = pe.matmul(ps[0:B, :], sc[:, k, :], wmod_sb[:, k, third * 2 * D:(third + 1) * 2 * D],
                                     start=(k == 0), stop=(k == KT - 1))
                last.then_inc(mod_psum, 1)

            def transpose_modulation(ps):
                for q in range(2):
                    for m in range(KT):
                        col = (3 + q) * D + m * P
                        at = (q * KT + m) * B
                        last = pe.transpose(ps[:, at:at + B], mod_rows[:, col:col + P], ident[0:B, 0:B])
                last.then_inc(modT_psum, 1)

            def transpose_rows(layer, b):
                pe.wait_ge(z_ready, B * layer + b + 1)
                for k in range(KT):
                    for t in range(2):
                        last = pe.transpose(zT_bank[layer][b][:, k * S + t * P:k * S + (t + 1) * P],
                                            z_rows(layer, 2 * b + t)[:, k * P:(k + 1) * P], ident[:, :])
                last.then_inc(zT_ready, 1)

            pe.wait_ge(silu_ready, 1)
            modulation_T(bank[7])
            pe.wait_ge(ident_in, 16)
            transpose_rows(0, 0)
            transpose_rows(0, 1)
            modulation(1, bank[6])

            def chunk(c, pair, half, i):
                ps = proj_bank[i % 3]
                if not (isinstance(c, int) and c < 3):
                    pe.wait_ge(chunk_lo, c - 2)
                if i in (0, 2):
                    pe.wait_ge(wqk_split, 2 * pair + (1 if i == 0 else 2))
                if i == 4:
                    pe.wait_ge(wv_split, pair + 1)
                if i < 4:
                    head, kind = i // 2, i % 2
                    cols = slice(half * HALF, (half + 1) * HALF)
                    for k in range(KT):
                        last = halves(pe, ps[:, :], [w[:, head, kind, k, :] for w in wqk],
                                      [t[:, k, cols] for t in hT], k == 0, k == KT - 1)
                else:
                    for j in range(2):
                        t = 4 * half + 2 * (i - 4) + j
                        for k in range(KT):
                            last = halves(pe, ps[:, j * 2 * DH:(j + 1) * 2 * DH],
                                          [h[:, k, t * P:(t + 1) * P] for h in hT],
                                          [w[:, k, :] for w in wv_s], k == 0, k == KT - 1)
                last.then_inc(chunk_ready, 1)

            def scores(n, c0, i):
                half, head, b = i // 4, i % 2, i // 2 % 2
                pe.wait_ge(chunk_lo, c0 + (2 if head == 0 else 4))
                if not (isinstance(n, int) and n < 2):
                    pe.wait_ge(masked, 2 * (n - 1))
                cols = slice(b * S, (b + 1) * S)
                for t in range(2):
                    last = halves(pe, score_bank[i % 2][:, t * S:(t + 1) * S],
                                  [q[:, half, head, 0, b * S + t * P:b * S + (t + 1) * P] for q in qkT],
                                  [q[:, half, head, 1, cols] for q in qkT], True, True)
                last.then_inc(scores_ready, 1)

            def transpose_probs(n, i):
                pe.wait_ge(softmax_ready, n + 1)
                if not (isinstance(n, int) and n < 1):
                    pe.wait_ge(pT_lo, n)
                pr = prob[:, i % 2, :, :]
                pe.transpose(pT_bank[:, 0:P], pr[:, 0, P:S], ident[:, :])
                pe.transpose(pT_bank[:, P:S], pr[:, 1, P:S], ident[:, :])
                pe.transpose(pT_bank[:, S:S + P], pr[:, 0, 0:P], ident[:, :])
                pe.transpose(pT_bank[:, S + P:S + REACH], pr[0:FAR, 1, 0:P], ident[0:FAR, 0:FAR])\
                  .then_inc(pT_ready, 1)

            def attend(n, c0, i):
                half, head, b = i // 4, i % 2, i // 2 % 2
                pe.wait_ge(chunk_lo, c0 + CHUNKS - 1 + b)
                pe.wait_ge(pT_lo, n + 1)
                if not (isinstance(n, int) and n < 1):
                    pe.wait_ge(oT_lo, n)
                t0 = 4 * half + 2 * b
                for slot, t in ((0, 1), (1, 0)):
                    last = halves(pe, oT_bank[:, 0:S],
                                  [w[:, t0 + t, head * DH:(head + 1) * DH] for w in v],
                                  [p[:, slot, :] for p in pT], slot == 0, slot == 1)
                last.then_inc(oT_ready, 1)

            def project_out(u, n_done, pair, i):
                pe.wait_ge(oT_lo, n_done)
                pe.wait_ge(wo_split, pair + 1)
                if not (isinstance(u, int) and u < 1):
                    pe.wait_ge(outp_added, u)
                else:
                    pe.wait_ge(modT_ready, 2)
                for t in range(2):
                    for head in range(2):
                        last = halves(pe, out_bank[:, t * D:(t + 1) * D],
                                      [o[:, i % 4 + head, t * P:(t + 1) * P] for o in oT],
                                      [w[:, head, :] for w in wo_s], head == 0, head == 1)
                last.then_inc(outp_ready, 1)

            pe.wait_ge(hT_ready, 2)
            for i in range(CHUNKS):
                chunk(i, 0, 0, i)
                if i == 4:
                    pe.wait_ge(mod_copied, 1)
                if i in (3, 4):
                    transpose_rows(0, i - 1)
            pe.wait_ge(zeros, 1)

            def pair_of_heads(pair, first_pair, last_pair):
                for i in range(UNITS):
                    n = UNITS * pair + i
                    seg = i // 4
                    c0 = 2 * CHUNKS * pair + CHUNKS * seg
                    c_seg = 0 if last_pair else seg
                    c_base, c_pair, c_half = 2 * CHUNKS * pair + CHUNKS * (c_seg + 1), pair + c_seg, 1 - c_seg
                    chunks, early = chunks_of(i, first_pair, last_pair)
                    scores(n, c0, i)
                    if first_pair and i == 0:
                        pe.wait_ge(modT_ready, 1)
                        modulation(2, bank[7])
                        pe.wait_ge(hT_ready, B)
                    if not (first_pair and i < 2):
                        attend(n - 2, c0 if i % 4 > 1 else c0 - CHUNKS, (i - 2) % UNITS)
                    for c in chunks[:early]:
                        chunk(c_base + c, c_pair, c_half, c)
                    if not (first_pair and i == 0):
                        transpose_probs(n - 1, i - 1)
                    if first_pair and i == 2:
                        pe.wait_ge(mod_copied, 2)
                        transpose_modulation(bank[7])
                    for c in chunks[early:]:
                        chunk(c_base + c, c_pair, c_half, c)
                    if i % 2 == 0 and not (first_pair and i < 4):
                        project_out(B * pair + (i - 4) // 2, n - 2, pair if i >= 4 else pair - 1, i)
                    if last_pair and i == 7:
                        transpose_rows(1, 0)

            pair_of_heads(0, True, False)
            with pe.Fori(1, PAIRS - 1) as pair:
                pair_of_heads(pair, False, False)
            pair_of_heads(PAIRS - 1, False, True)
            n_end = UNITS * PAIRS
            last_chunks = 2 * CHUNKS * PAIRS - CHUNKS
            attend(n_end - 2, last_chunks, UNITS - 2)
            transpose_probs(n_end - 1, 1)
            project_out(B * PAIRS - 2, n_end - 2, PAIRS - 1, 0)

            def gate_up(b, j):
                g = GROUPS * b + j
                pe.wait_ge(hT_ready, B + b + 1)
                if g == 0:
                    pe.wait_ge(wffn_split, FFN_PARTS * PAIRS)
                    pe.wait_ge(chunk_lo, 2 * CHUNKS * PAIRS)
                if g == 1:
                    pe.wait_ge(masked, 2 * UNITS * PAIRS)
                if g >= 2:
                    pe.wait_ge(gated_done, g - 1)
                for kind in range(2):
                    for m in range(2):
                        for k in range(KT):
                            col = (kind * KT + k) * F + (2 * j + m) * P
                            last = halves(pe, gu_banks[g % 2][kind][:, m * S:(m + 1) * S],
                                          [w[:, col:col + P] for w in wffn_s],
                                          [t[:, k, b * S:(b + 1) * S] for t in hT], k == 0, k == KT - 1)
                    last.then_inc(gu_ready, 1)

            def down(b, tiles):
                for t in tiles:
                    ps_bank, at = down_bank[2 * b + t]
                    for m in range(NM):
                        g = GROUPS * b + m // 2
                        pe.wait_ge(gated_lo, g + 1)
                        col = 2 * KT * F + m * D
                        tok = slice(m % 2 * S + t * P, m % 2 * S + (t + 1) * P)
                        last = halves(pe, ps_bank[:, at:at + D], [gated_slot(p, g)[:, tok] for p in (0, 1)],
                                      [w[:, col:col + D] for w in wffn_s], m == 0, m == NM - 1)
                last.then_inc(down_ready, 1)

            gate_up(0, 0)
            attend(n_end - 1, last_chunks, UNITS - 1)
            gate_up(0, 1)
            project_out(B * PAIRS - 1, n_end, PAIRS - 1, 2)
            for b in range(B):
                for j in range(2 if b == 0 else 0, GROUPS):
                    gate_up(b, j)
                    if j == 1 and b < B - 1:
                        down(b - 1, (0, 1))
                    if j == 2 and b < B - 1:
                        pe.wait_ge(haff_ready, B + b + 1)
                        transpose_rows(1, b + 1)
            pe.wait_ge(outp_added, B * PAIRS)
            down(B - 2, (0, 1))
            for t in range(2):
                pe.wait_ge(y_ready, 2 * t + 2)
                down(B - 1, (t,))

        @block.scalar
        def _(act):
            cols = (slice(0, 2 * D), slice(2 * D, 6 * D))
            act.dma_start(wmod_sb[:, :, cols[0]], wmod[:, :, cols[0]]).then_inc(wmod_in[0], 16)
            act.dma_start(ident[:, :], identity).then_inc(ident_in, 16)
            act.wait_ge(c_in, 16)
            act.activation(silu_c[:, 0, :], cT_sb[:, :, :].rearrange("p k b -> p (k b)"), ACT.Exp, scale=-1.0)\
               .then_inc(exp_c, 1)
            act.dma_start(wmod_sb[:, :, cols[1]], wmod[:, :, cols[1]]).then_inc(wmod_in[1], 16)
            act.dma_start(mask_sb[:, :], mask).then_inc(mask_in, 16)

            def modulate(layer, b):
                if layer == 0 and b == 0:
                    act.wait_ge(modT_ready, 1)
                act.wait_ge(zT_ready, B * layer + b + 1)
                if B * layer + b >= 2:
                    act.wait_ge(hT_ready, B * layer + b - 1)
                for k in range(KT):
                    last = act.activation(haff[:, b % 2, k, :], zT_bank[layer][b][:, k * S:(k + 1) * S],
                                          ACT.Identity, scale=modT[:, 2 * layer + 1, k, b:b + 1],
                                          bias=modT[:, 2 * layer, k, b:b + 1])
                last.then_inc(haff_ready, 1)
                act.wait_ge(haff_ready, B * layer + b + 1)
                act.activation(hT[0][:, :, b * S:(b + 1) * S], haff[:, b % 2, :, :], ACT.Copy).then_inc(hT_hi, 1)

            def copy_modulation(third, ps):
                act.wait_ge(mod_psum, third)
                act.activation(mod_rows[:, third * 2 * D:(third + 1) * 2 * D], ps[0:B, :], ACT.Copy)\
                   .then_inc(mod_copied, 1)

            modulate(0, 0)
            modulate(0, 1)
            copy_modulation(1, bank[6])

            def chunk_copy(c, half, i):
                act.wait_ge(chunk_ready, c + 1)
                ps = proj_bank[i % 3]
                if i < 4:
                    dst = qkT[0][:, half, i // 2, i % 2, :]
                else:
                    t = 4 * half + 2 * (i - 4)
                    dst = v[0][:, t:t + 2, :].rearrange("p a b -> p (a b)")
                act.activation(dst, ps[:, :], ACT.Copy).then_inc(chunk_hi, 1)

            def exps(n, i):
                for t, width in ((0, REACH), (1, S)):
                    act.wait_ge(masked, 2 * n + t + 1)
                    p = prob[:, i % 2, t, 0:width]
                    act.activation(p, p, ACT.Exp, bias=nmax[:, i % 2, t:t + 1], scale=-1.0,
                                   accum_out=rsum[:, i % 2, t:t + 1]).then_inc(exp_done, 1)

            def pT_copy(n):
                act.wait_ge(pT_ready, n + 1)
                act.activation(pT[0][:, :, :].rearrange("p a b -> p (a b)")[:, 0:S + REACH],
                               pT_bank[:, 0:S + REACH], ACT.Copy).then_inc(pT_hi, 1)

            for i in range(CHUNKS):
                chunk_copy(i, 0, i)
                if i in (3, 4):
                    modulate(0, i - 1)
            act.wait_ge(zeros, 1)

            def oT_unit(pair, j):
                n = UNITS * pair + j
                act.wait_ge(oT_ready, n + 1)
                if not (isinstance(pair, int) and UNITS * pair + j < 4):
                    act.wait_ge(outp_ready, B * pair + j // 2 - 1)
                act.activation(oT[0][:, j % 4, :], oT_bank[:, 0:S], ACT.Copy).then_inc(oT_hi, 1)

            def pair_of_heads(pair, first_pair, last_pair):
                for i in range(UNITS):
                    n = UNITS * pair + i
                    c_seg = 0 if last_pair else i // 4
                    c_base, c_half = 2 * CHUNKS * pair + CHUNKS * (c_seg + 1), 1 - c_seg
                    chunks = chunks_of(i, first_pair, last_pair)[0]
                    exps(n, i)
                    if first_pair and i == 0:
                        copy_modulation(2, bank[7])
                    if not (first_pair and i < 2):
                        oT_unit(pair, i - 2)
                    if not (first_pair and i == 0):
                        pT_copy(n - 1)
                    for c in chunks:
                        chunk_copy(c_base + c, c_half, c)
                    if first_pair and i == 4:
                        act.wait_ge(gates_row, 2)
                        g_rows = mod_rows[:, :].rearrange("b (a c d) -> b a c d", a=2, c=3)[:, :, 2, :]
                        act.dma_start(gates_dram.rearrange("b (g d) -> b g d", g=2), g_rows).then_inc(gates_out, 16)
                    if first_pair and i == 6:
                        act.wait_ge(gates_out, 16)
                        act.dma_start(gates_bc[:, :, :, :].rearrange("p b g d -> p (b g d)"),
                                      gates_dram.rearrange("b n -> (b n)").partition_broadcast(P))\
                           .then_inc(gates_in, 16)

            pair_of_heads(0, True, False)
            with act.Fori(1, PAIRS - 1) as pair:
                pair_of_heads(pair, False, False)
            pair_of_heads(PAIRS - 1, False, True)
            modulate(1, 0)
            oT_unit(PAIRS, -2)
            pT_copy(UNITS * PAIRS - 1)

            for g in range(B * GROUPS):
                act.wait_ge(gu_ready, 2 * g + 1)
                if g >= 2:
                    act.wait_ge(gated_done, g - 1)
                act.activation(tanh_g[:, g % 2, :], gu_banks[g % 2][0][:, :], ACT.Tanh, scale=0.5)\
                   .then_inc(tanh_done, 1)
                if g == 0:
                    oT_unit(PAIRS, -1)
                if g % GROUPS == 2 and g // GROUPS < B - 1:
                    modulate(1, g // GROUPS + 1)
                act.wait_ge(gated_done, g + 1)
                if g >= SLOTS:
                    act.wait_ge(down_ready, 1)
                act.activation(gated_slot(0, g), gated[:, g % 2, :], ACT.Copy).then_inc(gated_hi, 1)

        @block.vector
        def _(dve):
            chained = [0]

            def link(ins):
                chained[0] += 1
                ins.then_inc(chain_v, 1)
                dve.wait_ge(chain_v, chained[0])

            def ln_stats(t0, n, loads={}):
                for t in range(t0, t0 + n):
                    if t in loads:
                        dve.wait_ge(loads[t], 16)
                    last = dve.bn_stats(stats[:, t, :], x_sb[:, t, :])
                link(last)
                for t in range(t0, t0 + n):
                    last = dve.bn_aggr(mv[:, t, :], stats[:, t, :])
                link(last)
                dve.tensor_scalar(root[:, 4, t0:t0 + n], mv[:, t0:t0 + n, 0], -1.0, None, ALU.mult)
                link(dve.tensor_scalar(root[:, 0, t0:t0 + n], mv[:, t0:t0 + n, 1], EPS, None, ALU.add))

            def root_rows(t0, n):
                return [root[:, r, t0:t0 + n] for r in range(4)]

            def root_guess(t0, n):
                var, y, a, _ = root_rows(t0, n)
                link(dve.tensor_scalar(a.bitcast(I32), var.bitcast(I32), 1, None, ALU.logical_shift_right))
                link(dve.tensor_scalar(y.bitcast(I32), a.bitcast(I32), -1.0, ROOT_GUESS, ALU.mult, ALU.add))

            def root_step(t0, n):
                var, y, a, b = root_rows(t0, n)
                link(dve.tensor_tensor(a, y, y, ALU.mult))
                link(dve.scalar_tensor_tensor(b, a, -0.5, var, ALU.mult, ALU.mult))
                link(dve.scalar_tensor_tensor(y, b, 1.5, y, ALU.add, ALU.mult))

            def ln_root(t0, n):
                root_guess(t0, n)
                for _ in range(3):
                    root_step(t0, n)

            def ln_rows(layer, t0, n):
                for t in range(t0, t0 + n):
                    last = dve.tensor_scalar(z_rows(layer, t), x_sb[:, t, :], root[:, 4, t:t + 1],
                                             root[:, 1, t:t + 1], ALU.add, ALU.mult)
                    if t % 2 == 1:
                        last.then_inc(z_ready, 1)

            def h_lo(layer, b):
                dve.wait_ge(hT_hi, B * layer + b + 1)
                dve.tensor_tensor(hT[1][:, :, b * S:(b + 1) * S], haff[:, b % 2, :, :],
                                  f(hT[0][:, :, b * S:(b + 1) * S]), ALU.subtract).then_inc(hT_ready, 1)

            def copy_modT(j, ps):
                dve.wait_ge(modT_psum, j + 1)
                src = ps[:, 0:2 * KT * B].rearrange("p (q k b) -> p q k b", q=2, k=KT)
                dve.tensor_copy(modT[:, 2 * j, :, :], src[:, 0, :, :])
                dve.tensor_scalar(modT[:, 2 * j + 1, :, :], src[:, 1, :, :], 1.0, None, ALU.add)\
                   .then_inc(modT_ready, 1)

            dve.wait_ge(exp_c, 1)
            link(dve.tensor_scalar(silu_c[:, 1, :], silu_c[:, 0, :], 1.0, None, ALU.add))
            link(dve.reciprocal(silu_c[:, 0, :], silu_c[:, 1, :]))
            dve.tensor_tensor(silu_c[:, 2, :], silu_c[:, 0, :], cT_sb[:, :, :].rearrange("p k b -> p (k b)"),
                              ALU.mult).then_inc(silu_ready, 1)
            ln_stats(0, 4, {0: x_in[0], 2: x_in[1]})
            ln_root(0, 4)
            ln_rows(0, 0, 4)
            copy_modT(0, bank[7])
            h_lo(0, 0)
            h_lo(0, 1)

            def chunk_rest(c, half, i):
                dve.wait_ge(chunk_hi, c + 1)
                ps = proj_bank[i % 3]
                if i < 4:
                    hi, lo = (t[:, half, i // 2, i % 2, :] for t in qkT)
                else:
                    t0 = 4 * half + 2 * (i - 4)
                    hi, lo = (t[:, t0:t0 + 2, :].rearrange("p a b -> p (a b)") for t in v)
                dve.tensor_tensor(lo, ps[:, :], f(hi), ALU.subtract).then_inc(chunk_lo, 1)

            def oT_rest(pair, j):
                n = UNITS * pair + j
                dve.wait_ge(oT_hi, n + 1)
                dve.tensor_tensor(oT[1][:, j % 4, :], oT_bank[:, 0:S], f(oT[0][:, j % 4, :]), ALU.subtract)\
                   .then_inc(oT_lo, 1)

            def mask_scores(n, i):
                for t, width in ((0, REACH), (1, S)):
                    dve.tensor_tensor_reduce(out=prob[:, i % 2, t, 0:width],
                                             in0=score_bank[i % 2][:, t * S:t * S + width],
                                             in1=mask_sb[:, t * REACH:t * REACH + width],
                                             scale=-SCALE, scalar=3e38, op0=ALU.add, op1=ALU.min,
                                             accum_out=nmax[:, i % 2, t:t + 1]).then_inc(masked, 1)

            def invert_sums(n, i):
                dve.wait_ge(exp_done, 2 * n + 2)
                dve.reciprocal(rinv[:, i % 2, :], rsum[:, i % 2, :]).then_inc(rinv_ready, 1)

            def pT_rest(n):
                dve.wait_ge(pT_hi, n + 1)
                hi, lo = (t[:, :, :].rearrange("p a b -> p (a b)")[:, 0:S + REACH] for t in pT)
                dve.tensor_tensor(lo, pT_bank[:, 0:S + REACH], f(hi), ALU.subtract).then_inc(pT_lo, 1)

            def add_output(u, b):
                dve.wait_ge(outp_ready, u + 1)
                a = acc[:, 2 * b:2 * b + 2, :]
                dve.tensor_tensor(a, out_bank[:, :].rearrange("p (t d) -> p t d", t=2), a, ALU.add)\
                   .then_inc(outp_added, 1)

            ln_stats(4, 4, {4: x_in[2]})
            chunk_rest(0, 0, 0)
            ln_root(4, 4)
            ln_rows(0, 4, 2)
            chunk_rest(1, 0, 1)
            ln_rows(0, 6, 2)
            for i in range(2, CHUNKS):
                chunk_rest(i, 0, i)
            dve.wait_ge(zeros, 1)
            dve.wait_ge(mask_in, 16)

            def pair_of_heads(pair, first_pair, last_pair):
                for i in range(UNITS):
                    n = UNITS * pair + i
                    c_seg = 0 if last_pair else i // 4
                    c_base, c_half = 2 * CHUNKS * pair + CHUNKS * (c_seg + 1), 1 - c_seg
                    chunks = chunks_of(i, first_pair, last_pair)[0]
                    if not (first_pair and i < 2):
                        dve.wait_ge(pT_ready, n - 1)
                    dve.wait_ge(scores_ready, n + 1)
                    dve.memset(turn[:, :], 0.0)
                    mask_scores(n, i)
                    if last_pair and i == 6:
                        root_guess(0, 2)
                        root_step(0, 2)
                    if last_pair and i == 7:
                        ln_rows(1, 0, 2)
                    invert_sums(n, i)
                    if last_pair and i == 6:
                        root_step(0, 2)
                    if not (first_pair and i < 2):
                        oT_rest(pair, i - 2)
                    if not (first_pair and i == 0):
                        pT_rest(n - 1)
                    for c in chunks:
                        chunk_rest(c_base + c, c_half, c)
                    if first_pair and i == 2:
                        copy_modT(1, bank[7])
                    if first_pair and i == 3:
                        dve.wait_ge(acc_zero, 1)
                    if i % 2 == 0 and not (first_pair and i < 4):
                        add_output(B * pair + (i - 4) // 2, (i - 4) // 2 % B)
                    if last_pair and i == 5:
                        dve.wait_ge(x2_ready, 1)
                        ln_stats(0, 2)
                    if last_pair and i == 6:
                        root_step(0, 2)

            pair_of_heads(0, True, False)
            with dve.Fori(1, PAIRS - 1) as pair:
                pair_of_heads(pair, False, False)
            pair_of_heads(PAIRS - 1, False, True)
            oT_rest(PAIRS, -2)
            h_lo(1, 0)
            pT_rest(UNITS * PAIRS - 1)
            add_output(B * PAIRS - 2, 2)

            def finish(t, n):
                ps_bank, at = down_bank[t]
                ps = ps_bank[:, at:at + n * D].rearrange("p (t d) -> p t d", t=n)
                tiles = slice(t, t + n)
                g = gates_bc[:, t // 2:t // 2 + 1, 1, :].broadcast_to([P, n, D])
                link(dve.tensor_tensor(acc[:, tiles, :], ps, g, ALU.mult))
                dve.tensor_tensor(acc[:, tiles, :], acc[:, tiles, :], x_sb[:, tiles, :], ALU.add)\
                   .then_inc(y_ready, n)

            for g in range(B * GROUPS):
                b, j = g // GROUPS, g % GROUPS
                dve.wait_ge(tanh_done, g + 1)
                t = tanh_g[:, g % 2, :]
                link(dve.scalar_tensor_tensor(t, t, 1.0, gu_banks[g % 2][0][:, :], ALU.add, ALU.mult))
                dve.wait_ge(gu_ready, 2 * g + 2)
                if g >= 2:
                    dve.wait_ge(gated_lo, g - 1)
                dve.scalar_tensor_tensor(gated[:, g % 2, :], t, 0.5, gu_banks[g % 2][1][:, :],
                                         ALU.mult, ALU.mult).then_inc(gated_done, 1)
                if g == 0:
                    oT_rest(PAIRS, -1)
                    dve.wait_ge(x2_ready, 2)
                    ln_stats(2, 2)
                    ln_root(2, 2)
                    ln_rows(1, 2, 2)
                if g == 1:
                    add_output(B * PAIRS - 1, 3)
                if g == GROUPS + 1:
                    dve.wait_ge(x2_ready, B)
                    ln_stats(4, 4)
                    ln_root(4, 4)
                    dve.wait_ge(zT_ready, B + 2)
                    ln_rows(1, 4, 4)
                if j == 2 and b < B - 1:
                    h_lo(1, b + 1)
                    if b > 0:
                        dve.wait_ge(down_ready, b)
                        finish(2 * b - 2, 2)
            dve.wait_ge(down_ready, B - 1)
            finish(NT - 4, 2)
            for t in (NT - 2, NT - 1):
                dve.wait_ge(down_ready, B + t - (NT - 2))
                finish(t, 1)


_OUTS = [((P, NT, D), "float32")]


def kernel(**inputs):
    import numpy as _np
    import concourse.bacc as _bacc
    from concourse import mybir as _mybir
    from concourse.bass_utils import run_bass_kernel_spmd as _run

    a = {name.removeprefix("L0_"): _np.asarray(value) for name, value in inputs.items()}
    def by_partition(w):
        return w.reshape(-1, P, w.shape[1]).transpose(1, 0, 2)

    qk = _np.stack([by_partition(a["attn_Wq"]), by_partition(a["attn_Wk"])], axis=1)
    qk = qk.reshape(P, 2, KT, PAIRS, 2, DH).transpose(0, 3, 4, 1, 2, 5).reshape(P, PAIRS, -1)
    wv = by_partition(a["attn_Wv"]).reshape(P, KT, PAIRS, 2 * DH).transpose(0, 2, 1, 3).reshape(P, PAIRS, -1)
    wo = by_partition(a["attn_Wo"]).reshape(P, PAIRS, 2 * D)
    wattn = _np.concatenate([qk, wv, wo], axis=2).reshape(P, -1)
    wffn = _np.concatenate([by_partition(w.T).reshape(P, -1)
                            for w in (a["ffn_w_gate"], a["ffn_w_up"], a["ffn_w_down"])], axis=1)
    order = _np.array(token_order())
    x = a["attn_hidden_states"][:, order, :].reshape(NT, P, D).transpose(1, 0, 2)
    q, k = order[:, None], order[None, :]
    seen = (_np.abs(q - k) < WINDOW) | (q < GLOBAL) | (k < GLOBAL)
    full = _np.where(seen, 0.0, MASKED).astype(_np.float32)
    mask = _np.concatenate([full[:P, :REACH], full[P:, :]], axis=1)

    nc = _bacc.Bacc("TRN2", target_bir_lowering=False, num_devices=1)
    named = [("x", x), ("wattn", wattn), ("wffn", wffn), ("cT", by_partition(a["c"].T)),
             ("wmod", by_partition(a["wmod"])), ("mask", mask), ("identity", _np.eye(P, dtype=_np.float32))]
    arrays, args = {}, []
    for name, value in named:
        value = _np.ascontiguousarray(value)
        arrays[f"in_{name}"] = value
        args.append(nc.dram_tensor(f"in_{name}", value.shape, _mybir.dt.from_np(value.dtype),
                                   kind="ExternalInput").ap())
    for i, (shape, dtype) in enumerate(_OUTS):
        args.append(nc.dram_tensor(f"out_{i}", shape, _mybir.dt.from_np(_np.dtype(dtype)),
                                   kind="ExternalOutput").ap())
    adaln_block_kernel(nc, *args)
    r = _run(nc, [arrays], core_ids=[0])
    y = _np.empty((B, S, D), _np.float32)
    y[:, order, :] = _np.asarray(r.results[0]["out_0"]).transpose(1, 0, 2).reshape(B, S, D)
    return y
```
